# Optimizing a Trainium2 kernel written in Bass

```python
import numpy as np
import jax
import jax.numpy as jnp

def _softmax(x, axis=-1):
    return jax.nn.softmax(x, axis=axis)

def _gelu(x):
    return jax.nn.gelu(x, approximate=True)

def _silu(x):
    return jax.nn.silu(x)

def _sigmoid(x):
    return jax.nn.sigmoid(x)

def _layernorm(x, axis=-1, eps=1e-05):
    m = jnp.mean(x, axis=axis, keepdims=True)
    v = jnp.var(x, axis=axis, keepdims=True)
    return (x - m) / jnp.sqrt(v + eps)

def _scatter_add(tgt, idx, src, axis=0):
    return tgt.at[idx].add(src)

def _segment_sum(src, seg, n):
    return jax.ops.segment_sum(src, seg, n)
kernel_name = 'mk_perceiver_d1_seqx_r8_eabc8b'

def setup_inputs(seed: int=0):
    np.random.seed(seed)
    _w = jnp.asarray

    def _rec_inputs():
        import jax
        import jax.numpy as jnp
        _rk = jax.random.key(seed)
        x = -0.0003929 + 0.9999 * jax.random.normal(jax.random.fold_in(_rk, 1), (2, 128, 256), jnp.float32)
        _lenS = 128 - jax.random.randint(jax.random.fold_in(_rk, 7), (2,), 0, max(1, 128 // 4) + 1, jnp.int32)
        _lenS2 = 2048 - jax.random.randint(jax.random.fold_in(_rk, 8), (2,), 0, max(1, 2048 // 4) + 1, jnp.int32)
        _ctx_1024P = jax.random.normal(jax.random.fold_in(_rk, 11), (2, 16, 128), jnp.float32)
        _ctx_1024c = jax.random.dirichlet(jax.random.fold_in(_rk, 511), 0.3 * jnp.ones((16,), jnp.float32), (2, 2048))
        _ctx_1024t = jnp.einsum('bsk,bkd->bsd', _ctx_1024c, _ctx_1024P)
        _ctx_1024t = _ctx_1024t * jax.lax.rsqrt(jnp.mean(jnp.square(_ctx_1024t)) + 1e-12) * 0.953939
        ctx_1024 = -0.000494167 + 1.00018 * (_ctx_1024t + 0.3 * jax.random.normal(jax.random.fold_in(_rk, 611), (2, 2048, 128), jnp.float32))
        _validS = jnp.arange(128)[None, :] < _lenS[:, None]
        _validS2 = jnp.arange(2048)[None, :] < _lenS2[:, None]
        _causal = jnp.tril(jnp.ones((128, 128), dtype=bool))
        mask_BxS2_bf1 = jnp.ones((2, 2048), dtype=bool)
        return (x, ctx_1024, mask_BxS2_bf1)
    x, ctx_1024, mask_BxS2_bf1 = _rec_inputs()

    def _L0_xattn_setup():
        import jax, jax.numpy as jnp
        import numpy as np
        N_HEADS = 16
        N_KV_HEADS = 8
        HEAD_DIM = 128
        D_TEXT = 256
        D_VISION = 128
        GROUPS = N_HEADS // N_KV_HEADS
        key = jax.random.key(seed)
        ks = jax.random.split(key, 6)
        B, T_text, T_vis = (4, 256, 72)
        text_hidden = jax.random.normal(ks[0], (B, T_text, D_TEXT), dtype=jnp.float32)
        vision_tokens = jax.random.normal(ks[1], (B, T_vis, D_VISION), dtype=jnp.float32)
        vision_mask = jnp.ones((B, T_vis), dtype=bool)
        s = 0.02
        Wq = jax.random.normal(ks[2], (D_TEXT, N_HEADS * HEAD_DIM), dtype=jnp.float32) * s
        Wk = jax.random.normal(ks[3], (D_VISION, N_KV_HEADS * HEAD_DIM), dtype=jnp.float32) * s
        Wv = jax.random.normal(ks[4], (D_VISION, N_KV_HEADS * HEAD_DIM), dtype=jnp.float32) * s
        Wo = jax.random.normal(ks[5], (N_HEADS * HEAD_DIM, D_TEXT), dtype=jnp.float32) * s
        return {'text_hidden': text_hidden, 'vision_tokens': vision_tokens, 'vision_mask': vision_mask, 'Wq': Wq, 'Wk': Wk, 'Wv': Wv, 'Wo': Wo}
    _L0_xattn_all = _L0_xattn_setup()
    _L0_xattn_in = {k: v for k, v in _L0_xattn_all.items() if k in ('Wq', 'Wk', 'Wv', 'Wo')}
    del _L0_xattn_all

    def _L0_attn_setup():
        import jax, jax.numpy as jnp
        import numpy as np
        B, SQ, HIDDEN = (2, 256, 256)
        HEADS, GROUPS, KVC = (16, 4, 128)
        HPG = HEADS // GROUPS
        LAYER_INDEX = 1
        SCALE = KVC ** (-0.5)
        key = jax.random.key(seed)
        k1, k2, k3, k4 = jax.random.split(key, 4)
        return {'x': jax.random.normal(k1, (B, SQ, HIDDEN), jnp.float32), 'w_q': jax.random.normal(k2, (HIDDEN, HEADS * KVC), jnp.float32) * 0.02, 'w_kv': jax.random.normal(k3, (HIDDEN, 2 * GROUPS * KVC), jnp.float32) * 0.02, 'w_dense': jax.random.normal(k4, (HEADS * KVC, HIDDEN), jnp.float32) * 0.02}
    _L0_attn_all = _L0_attn_setup()
    _L0_attn_in = {k: v for k, v in _L0_attn_all.items() if k in ('w_q', 'w_kv', 'w_dense')}
    del _L0_attn_all

    def _L0_ffn_setup():
        import jax, jax.numpy as jnp
        import numpy as np
        B, S, H = (1, 128, 256)
        F = 128
        E = 16
        K = 2
        NS = 1
        ROUTE_SCALE = 1.0
        key = jax.random.key(seed)
        ks = jax.random.split(key, 8)

        def w(k, shape, fan_in):
            return jax.random.normal(k, shape, jnp.float32) * fan_in ** (-0.5)
        return {'hidden_states': jax.random.normal(ks[0], (B, S, H), jnp.float32), 'gate_w': w(ks[1], (H, E), H), 'expert_bias': jnp.zeros((E,), jnp.float32), 'shared_gate_w': w(ks[2], (H, F * NS), H), 'shared_up_w': w(ks[3], (H, F * NS), H), 'shared_down_w': w(ks[4], (F * NS, H), F * NS), 'experts_gate_up': w(ks[5], (E, H, 2 * F), H), 'experts_down': w(ks[6], (E, F, H), F)}
    _L0_ffn_all = _L0_ffn_setup()
    _L0_ffn_in = {k: v for k, v in _L0_ffn_all.items() if k in ('gate_w', 'expert_bias', 'shared_gate_w', 'shared_up_w', 'shared_down_w', 'experts_gate_up', 'experts_down')}
    del _L0_ffn_all
    return {'x': x, 'ctx_1024': ctx_1024, 'mask_BxS2_bf1': mask_BxS2_bf1, 'L0_xattn_Wq': _L0_xattn_in['Wq'], 'L0_xattn_Wk': _L0_xattn_in['Wk'], 'L0_xattn_Wv': _L0_xattn_in['Wv'], 'L0_xattn_Wo': _L0_xattn_in['Wo'], 'L0_attn_w_q': _L0_attn_in['w_q'], 'L0_attn_w_kv': _L0_attn_in['w_kv'], 'L0_attn_w_dense': _L0_attn_in['w_dense'], 'L0_ffn_gate_w': _L0_ffn_in['gate_w'], 'L0_ffn_expert_bias': _L0_ffn_in['expert_bias'], 'L0_ffn_shared_gate_w': _L0_ffn_in['shared_gate_w'], 'L0_ffn_shared_up_w': _L0_ffn_in['shared_up_w'], 'L0_ffn_shared_down_w': _L0_ffn_in['shared_down_w'], 'L0_ffn_experts_gate_up': _L0_ffn_in['experts_gate_up'], 'L0_ffn_experts_down': _L0_ffn_in['experts_down']}

def reference(x, ctx_1024, mask_BxS2_bf1, L0_xattn_Wq, L0_xattn_Wk, L0_xattn_Wv, L0_xattn_Wo, L0_attn_w_q, L0_attn_w_kv, L0_attn_w_dense, L0_ffn_gate_w, L0_ffn_expert_bias, L0_ffn_shared_gate_w, L0_ffn_shared_up_w, L0_ffn_shared_down_w, L0_ffn_experts_gate_up, L0_ffn_experts_down):
    import jax
    import jax.numpy as jnp

    def _L0_xattn_ref(text_hidden, vision_tokens, vision_mask, Wq, Wk, Wv, Wo):
        import jax, jax.numpy as jnp
        import numpy as np
        N_HEADS = 16
        N_KV_HEADS = 8
        HEAD_DIM = 128
        D_TEXT = 256
        D_VISION = 128
        GROUPS = N_HEADS // N_KV_HEADS
        B, T_text, _ = text_hidden.shape
        T_vis = vision_tokens.shape[1]
        scale = jnp.float32(np.sqrt(HEAD_DIM))
        q = (text_hidden @ Wq).reshape(B, T_text, N_HEADS, HEAD_DIM).transpose(0, 2, 1, 3)
        k = (vision_tokens @ Wk).reshape(B, T_vis, N_KV_HEADS, HEAD_DIM).transpose(0, 2, 1, 3)
        v = (vision_tokens @ Wv).reshape(B, T_vis, N_KV_HEADS, HEAD_DIM).transpose(0, 2, 1, 3)
        k = jnp.repeat(k, GROUPS, axis=1)
        v = jnp.repeat(v, GROUPS, axis=1)
        scores = jnp.einsum('bhtd,bhsd->bhts', q, k) / scale
        mask = vision_mask[:, None, None, :]
        scores = jnp.where(mask, scores, -jnp.inf)
        attn = jax.nn.softmax(scores, axis=-1)
        attn = jnp.nan_to_num(attn, nan=0.0)
        out = jnp.einsum('bhts,bhsd->bhtd', attn, v)
        out = out.transpose(0, 2, 1, 3).reshape(B, T_text, N_HEADS * HEAD_DIM)
        return out @ Wo

    def _L0_attn_ref(x, w_q, w_kv, w_dense):
        import jax, jax.numpy as jnp
        import numpy as np
        B, SQ, HIDDEN = (2, 256, 256)
        HEADS, GROUPS, KVC = (16, 4, 128)
        HPG = HEADS // GROUPS
        LAYER_INDEX = 1
        SCALE = KVC ** (-0.5)
        b, sq, _ = x.shape
        sk = sq
        q = jnp.einsum('bsh,he->bse', x, w_q).reshape(b, sq, GROUPS, HPG, KVC)
        kv = jnp.einsum('bsh,he->bse', x, w_kv)
        k, v = jnp.split(kv, 2, axis=-1)
        k = k.reshape(b, sk, GROUPS, KVC)
        v = v.reshape(b, sk, GROUPS, KVC)
        scores = jnp.einsum('bqgpd,bkgd->bgqpk', q, k) * (SCALE / LAYER_INDEX)
        scores = scores.astype(jnp.float32) * LAYER_INDEX
        causal = jnp.arange(sq)[:, None] >= jnp.arange(sk)[None, :]
        scores = jnp.where(causal[None, None, :, None, :], scores, -jnp.inf)
        probs = jax.nn.softmax(scores, axis=-1).astype(x.dtype)
        ctx = jnp.einsum('bgqpk,bkgd->bqgpd', probs, v).reshape(b, sq, HEADS * KVC)
        return jnp.einsum('bse,eh->bsh', ctx, w_dense)

    def _L0_ffn_ref(hidden_states, gate_w, expert_bias, shared_gate_w, shared_up_w, shared_down_w, experts_gate_up, experts_down):
        import jax, jax.numpy as jnp
        import numpy as np
        B, S, H = (1, 128, 256)
        F = 128
        E = 16
        K = 2
        NS = 1
        ROUTE_SCALE = 1.0
        b, s, h = hidden_states.shape
        x = hidden_states.reshape(-1, h)
        T = x.shape[0]
        router_logits = (x @ gate_w).astype(jnp.float32)
        scores = jax.nn.sigmoid(router_logits)
        _, selected = jax.lax.top_k(scores + expert_bias[None, :], K)
        top_scores = jnp.take_along_axis(scores, selected, axis=1)
        top_scores = top_scores / (top_scores.sum(-1, keepdims=True) + 1e-20)
        top_scores = top_scores * ROUTE_SCALE
        shared = jax.nn.silu(x @ shared_gate_w) * (x @ shared_up_w) @ shared_down_w
        comb = jnp.zeros((T, E), jnp.float32).at[jnp.arange(T)[:, None], selected].add(top_scores)
        routed = jnp.zeros_like(x)
        for e in range(E):
            gu = x @ experts_gate_up[e]
            g, u = jnp.split(gu, 2, axis=-1)
            routed = routed + comb[:, e:e + 1] * (jax.nn.silu(g) * u @ experts_down[e])
        return (shared + routed).reshape(b, s, h)
    x = x + _L0_xattn_ref(_layernorm(x, axis=-1), ctx_1024, mask_BxS2_bf1, L0_xattn_Wq, L0_xattn_Wk, L0_xattn_Wv, L0_xattn_Wo)
    x = x + _L0_attn_ref(_layernorm(x, axis=-1), L0_attn_w_q, L0_attn_w_kv, L0_attn_w_dense)
    x = x + _L0_ffn_ref(_layernorm(x, axis=-1), L0_ffn_gate_w, L0_ffn_expert_bias, L0_ffn_shared_gate_w, L0_ffn_shared_up_w, L0_ffn_shared_down_w, L0_ffn_experts_gate_up, L0_ffn_experts_down)
    return x

_drawn_inputs = setup_inputs


def setup_inputs(seed=0):
    import zlib

    import numpy as np

    out = dict(_drawn_inputs(seed))
    spreads = {'L0_ffn_expert_bias': (0.0, 0.1)}
    factors = {'L0_xattn_Wq': 3.14, 'L0_xattn_Wk': 3.142}
    for name, (base, spread) in spreads.items():
        noise = np.random.default_rng([zlib.crc32(name.encode()), seed]).standard_normal(out[name].shape)
        drawn = base * np.exp(spread * noise) if base else spread * noise
        out[name] = jnp.asarray(drawn.astype(out[name].dtype))
    for name, factor in factors.items():
        out[name] = (out[name] * factor).astype(out[name].dtype)
    return out
```

```python
from contextlib import ExitStack

import concourse.bass as bass
from concourse import mybir

ALU = mybir.AluOpType
ACT = mybir.ActivationFunctionType
AX = mybir.AxisListType
F32 = mybir.dt.float32
F32R = mybir.dt.float32r
U8 = mybir.dt.uint8

P = 128
NEG = -1e38
EPS = 1e-5


def after(eng, sem, value):
    if not isinstance(value, int) or value > 0:
        eng.wait_ge(sem, value)


def perceiver_layer(nc, x, ctx_tokens, key_mask, xq_w, xk_w, xv_w, xo_w, sq_w, skv_w, sd_w,
                    gate_w, expert_bias, sh_gate_w, sh_up_w, sh_down_w, ex_gu_w, ex_down_w, out):
    B, T, H = x.shape
    _, KEYS, VIS = ctx_tokens.shape
    assert B == 2 and T == P and VIS == P and H == 2 * P
    HB = H // P
    XH = xq_w.shape[1] // P
    G = xk_w.shape[1] // P
    J = XH // G
    NBLK = KEYS // P
    CH = 512
    NCH = KEYS // CH
    SCALE = float(P) ** -0.5
    SH = sq_w.shape[1] // P
    R = skv_w.shape[1] // (2 * P)
    HR = SH // R
    E = gate_w.shape[1]
    F = ex_down_w.shape[1]
    RING = 4
    assert J == 2 and NCH == 4 and HR == 4 and F == P and E % RING == 0

    SPU = J * NCH
    STEPS = 2 * SPU
    LAG_T = SPU + 2
    LAG_A = LAG_T + 2
    NT = G * STEPS
    PTR = 4

    xq_v = xq_w.rearrange("(k p) (g e) -> g p k e", p=P, g=G)
    xk_v = xk_w.rearrange("p (g e) -> g p e", g=G)
    xv_v = xv_w.rearrange("p (g e) -> g p e", g=G)
    xo_v = xo_w.rearrange("(g j p) n -> g p j n", p=P, g=G)
    sq_v = sq_w.rearrange("(k p) (r e) -> r p k e", p=P, r=R)
    skv_v = skv_w.rearrange("(k p) (s r e) -> r s p k e", p=P, s=2, r=R)
    sd_v = sd_w.rearrange("(r h p) n -> r p h n", p=P, r=R)
    exgu_v = ex_gu_w.rearrange("e (k p) f -> e p k f", p=P)
    x_v = x.rearrange("b t d -> t b d")
    out_v = out.rearrange("b t d -> t b d")
    ctx_v = ctx_tokens.rearrange("b (p i) d -> b p (i d)", p=P)

    with ExitStack() as stack:
        def sb(name, shape, dt=F32):
            return stack.enter_context(nc.sbuf_tensor(name, shape, dt))

        def sem(name):
            return stack.enter_context(nc.semaphore(name))

        resid = sb("resid", [P, B, H])
        xn = sb("xn", [P, B, H])
        xnT = sb("xnT", [P, HB, B * T])
        ident = sb("ident", [P, P])
        causal = sb("causal", [P, P])
        minus_half = sb("minus_half", [P, 1])
        ctx_raw = sb("ctx_raw", [P, B * KEYS])
        ctx_hi = sb("ctx_hi", [P, B, NBLK, P], F32R)
        ctx_lo = sb("ctx_lo", [P, B, NBLK, P], F32R)
        ctxT_hi = sb("ctxT_hi", [P, B, KEYS], F32R)
        ctxT_lo = sb("ctxT_lo", [P, B, KEYS], F32R)
        mask8 = sb("mask8", [P, B, KEYS], U8)
        mask_bias = sb("mask_bias", [P, B, KEYS])
        probs = sb("probs", [P, B, J, KEYS])
        pT_hi = sb("pT_hi", [P, PTR, CH], F32R)
        pT_lo = sb("pT_lo", [P, PTR, CH], F32R)
        wq = sb("wq", [P, HB, J * P])
        wk = sb("wk", [P, P])
        wv = sb("wv", [P, P])
        wo = sb("wo", [P, J, H])
        wkT = sb("wkT", [P, P])
        qT = sb("qT", [P, B, J, T])
        qk_hi = sb("qk_hi", [P, B, J, T], F32R)
        qk_lo = sb("qk_lo", [P, B, J, T], F32R)
        oT = sb("oT", [P, J * T])
        yT = sb("yT", [P, J, T])
        stats = sb("stats", [P, B, 6])
        meanvar = sb("meanvar", [P, B, 2])
        var_eps = sb("var_eps", [P, B, 1])
        rstd = sb("rstd", [P, B, 1])
        rmax = sb("rmax", [P, B, J, NCH])
        negmax = sb("negmax", [P, B, J])
        den = sb("den", [P, B, J, 2])
        dsum = sb("dsum", [P, B, J])
        rden = sb("rden", [P, B, J])
        ring_gu = sb("ring_gu", [P, RING, HB, 2 * F])
        ring_dn = sb("ring_dn", [P, RING, H])
        gatew = sb("gatew", [P, HB, E])
        bias_b = sb("bias_b", [P, 1, E])
        rank = sb("rank", [P, 1, E])
        route = sb("route", [P, 10, B, E])
        r1 = sb("r1", [P, 6, B, 1])

        wq2 = ctx_raw[:, 0:1024].rearrange("p (k e) -> p k e", k=HB)
        wkv2 = ctx_raw[:, 1024:1536].rearrange("p (k s e) -> p k s e", k=HB, s=2)
        wd2 = ctx_raw[:, 1536:2560].rearrange("p (h n) -> p h n", h=HR)
        work = probs[:].rearrange("p b j k -> p (b j k)")
        q2T = work[:, 0:1024].rearrange("p (h t) -> p h t", h=HR)
        k2T = work[:, 1024:1280]
        v2 = work[:, 1280:1536].rearrange("p (b d) -> p b d", b=B)
        p2 = work[:, 1536:2560].rearrange("p (b h k) -> p b h k", b=B, h=HR)
        p2T = work[:, 2560:3584].rearrange("p (b n) -> p b n", b=B)
        c2T = work[:, 3584:4608].rearrange("p (b n) -> p b n", b=B)
        nm2 = work[:, 4608:4616].rearrange("p (b h) -> p b h", b=B)
        ds2 = work[:, 4624:4632].rearrange("p (b h) -> p b h", b=B)
        rd2 = work[:, 4640:4648].rearrange("p (b h) -> p b h", b=B)
        sg = work[:, 5120:5632].rearrange("p (s t) -> p s t", s=2)
        hT = work[:, 5632:6144].rearrange("p (s t) -> p s t", s=2)

        bank = [stack.enter_context(nc.psum_tensor(f"bank{i}", [P, CH], F32)) for i in range(8)]
        S_BANK, PT_BANK, O_BANK = bank[0:2], bank[2:4], bank[4:6]
        WQK_BANK, QYO_BANK = bank[6], bank[7]

        ld_x = sem("ld_x")
        ld_ctx = [sem(f"ld_ctx{i}") for i in range(B * NCH)]
        ld_mask = sem("ld_mask")
        ld_wq, ld_wk, ld_wv, ld_wo = sem("ld_wq"), sem("ld_wk"), sem("ld_wv"), sem("ld_wo")
        consts = sem("consts")
        mask_ready = sem("mask_ready")
        ln_stat, ln_pow, xn_ready = sem("ln_stat"), sem("ln_pow"), sem("xn_ready")
        xnT_psum, xnT_ready = sem("xnT_psum"), sem("xnT_ready")
        ctxT_psum, ctxT_hi_ready, ctxT_lo_ready = sem("ctxT_psum"), sem("ctxT_hi_ready"), sem("ctxT_lo_ready")
        ctx_hi_ready, ctx_lo_ready = sem("ctx_hi_ready"), sem("ctx_lo_ready")
        wkT_psum, wkT_ready = sem("wkT_psum"), sem("wkT_ready")
        q_psum, q_ready = sem("q_psum"), sem("q_ready")
        qk_psum, qk_hi_ready, qk_lo_ready = sem("qk_psum"), sem("qk_hi_ready"), sem("qk_lo_ready")
        scores, masked, negmax_ready, exps = sem("scores"), sem("masked"), sem("negmax_ready"), sem("exps")
        pT_psum, pT_hi_ready, pT_lo_ready = sem("pT_psum"), sem("pT_hi_ready"), sem("pT_lo_ready")
        av = sem("av")
        rden_step = sem("rden_step")
        oT_ready, y_psum, yT_ready, out_psum, added = (
            sem("oT_ready"), sem("y_psum"), sem("yT_ready"), sem("out_psum"), sem("added"))
        ld_wq2, ld_wk2, ld_wv2, ld_wd2 = sem("ld_wq2"), sem("ld_wk2"), sem("ld_wv2"), sem("ld_wd2")
        qa_psum, qb_psum, k2_psum, v2_psum = sem("qa_psum"), sem("qb_psum"), sem("k2_psum"), sem("v2_psum")
        qa_ready, qb_ready, k2_ready, v2_ready = sem("qa_ready"), sem("qb_ready"), sem("k2_ready"), sem("v2_ready")
        s2_psum, s2_masked, s2_negmax, s2_exps, s2_rden, s2_probs = (
            sem("s2_psum"), sem("s2_masked"), sem("s2_negmax"), sem("s2_exps"), sem("s2_rden"), sem("s2_probs"))
        p2T_psum, p2T_ready, c2_psum, c2_ready, d2_psum, added2 = (
            sem("p2T_psum"), sem("p2T_ready"), sem("c2_psum"), sem("c2_ready"), sem("d2_psum"), sem("added2"))
        ld_gate = sem("ld_gate")
        ld_ring = [sem(f"ld_ring{i}") for i in range(RING)]
        logits, gate_exp, route_step = sem("logits"), sem("gate_exp"), sem("route_step")
        gu_psum, silu_ready, h_ready, down_psum, added3 = (
            sem("gu_psum"), sem("silu_ready"), sem("h_ready"), sem("down_psum"), sem("added3"))
        stored = sem("stored")

        block = stack.enter_context(nc.Block())

        @block.sync
        def _(sp):
            sp.dma_start(resid[:], x_v).then_inc(ld_x, 16)

            def load_q(g):
                after(sp, q_psum, g)
                sp.dma_start(wq[:], xq_v[g]).then_inc(ld_wq, 16)
                after(sp, wkT_psum, g)
                sp.dma_start(wk[:], xk_v[g]).then_inc(ld_wk, 16)

            def load_o(g):
                after(sp, out_psum, 2 * g)
                sp.dma_start(wv[:], xv_v[g]).then_inc(ld_wv, 16)
                sp.dma_start(wo[:], xo_v[g]).then_inc(ld_wo, 16)

            load_q(0)
            sp.dma_start(mask8[:].rearrange("p b k -> p (b k)"),
                         key_mask.rearrange("(a b) k -> a (b k)", a=1).broadcast_to([P, B * KEYS])
                         ).then_inc(ld_mask, 16)
            load_o(0)
            sp.dma_start(gatew[:], gate_w.rearrange("(k p) e -> p k e", p=P)).then_inc(ld_gate, 16)
            sp.dma_start(bias_b[:, 0, :], expert_bias.rearrange("(a e) -> a e", a=1).broadcast_to([P, E])
                         ).then_inc(ld_gate, 16)
            load_q(1)
            with sp.Fori(1, G - 1) as g:
                load_q(g + 1)
                load_o(g)
            load_o(G - 1)

            sp.wait_ge(ctxT_psum, B * NCH)
            sp.wait_ge(ctx_hi_ready, B)
            sp.wait_ge(ctx_lo_ready, B)

            def load_s(r):
                after(sp, qa_psum, r)
                after(sp, qb_psum, r)
                sp.dma_start(wq2, sq_v[r]).then_inc(ld_wq2, 16)
                after(sp, k2_psum, r)
                sp.dma_start(wkv2[:, :, 0, :], skv_v[r, 0]).then_inc(ld_wk2, 16)
                after(sp, v2_psum, r)
                sp.dma_start(wkv2[:, :, 1, :], skv_v[r, 1]).then_inc(ld_wv2, 16)

            def load_d(r):
                after(sp, d2_psum, 2 * r)
                sp.dma_start(wd2, sd_v[r]).then_inc(ld_wd2, 16)

            load_s(0)
            load_d(0)
            sp.dma_start(ring_gu[:, 0, :, 0:F], sh_gate_w.rearrange("(k p) f -> p k f", p=P)).then_inc(ld_ring[0], 16)
            sp.dma_start(ring_gu[:, 0, :, F:2 * F], sh_up_w.rearrange("(k p) f -> p k f", p=P)).then_inc(ld_ring[0], 16)
            sp.dma_start(ring_dn[:, 0, :], sh_down_w).then_inc(ld_ring[0], 16)
            for m in range(1, RING):
                sp.dma_start(ring_gu[:, m], exgu_v[m - 1]).then_inc(ld_ring[m], 16)
                sp.dma_start(ring_dn[:, m, :], ex_down_w[m - 1]).then_inc(ld_ring[m], 16)
            load_s(1)
            with sp.Fori(1, R - 1) as r:
                load_s(r + 1)
                load_d(r)
            load_d(R - 1)

            def load_expert(i, s):
                sp.wait_ge(down_psum, RING * i + s - RING + 1)
                sp.dma_start(ring_gu[:, s], exgu_v[RING * i + s - 1]).then_inc(ld_ring[s], 16)
                sp.dma_start(ring_dn[:, s, :], ex_down_w[RING * i + s - 1]).then_inc(ld_ring[s], 16)

            with sp.Fori(1, E // RING) as i:
                for s in range(RING):
                    load_expert(i, s)
            load_expert(E // RING, 0)

            for b in range(B):
                sp.wait_ge(added3, B * E + b + 1)
                sp.dma_start(out_v[:, b, :], resid[:, b, :]).then_inc(stored, 16)
            sp.wait_ge(stored, 16 * B)

        @block.gpsimd
        def _(pool):
            pool.memset(ident[:], 0.0).then_inc(consts, 1)
            pool.memset(causal[:], 0.0).then_inc(consts, 1)
            pool.memset(minus_half[:], -0.5).then_inc(consts, 1)
            pool.iota(rank[:, 0, :], [[-1, E]], base=E, channel_multiplier=0,
                      allow_small_or_imprecise_dtypes=True).then_inc(consts, 1)
            pool.wait_ge(consts, 4)
            pool.affine_select(out=ident[:], in_=ident[:], compare_op=ALU.not_equal, fill=1.0, base=0,
                               pattern=[[-1, P]], channel_multiplier=1).then_inc(consts, 1)
            pool.affine_select(out=causal[:], in_=causal[:], compare_op=ALU.is_ge, fill=NEG, base=0,
                               pattern=[[-1, P]], channel_multiplier=1).then_inc(consts, 1)

            def power(b, n):
                pool.wait_ge(ln_stat, 3 * (B * n + b + 1))
                pool.tensor_tensor(rstd[:, b], var_eps[:, b], minus_half[:], ALU.pow).then_inc(ln_pow, 1)

            power(0, 0)
            power(1, 0)
            for b in range(B):
                if b == 0:
                    pool.wait_ge(ld_mask, 16)
                pool.tensor_scalar(mask_bias[:, b].rearrange("p (i q) -> p i q", i=NBLK),
                                   mask8[:, b].rearrange("p (q i) -> p i q", i=NBLK),
                                   -1.0, -NEG, ALU.add, ALU.mult).then_inc(mask_ready, 1)
                pool.wait_ge(ctx_hi_ready, b + 1)
                pool.tensor_tensor(ctx_lo[:, b].rearrange("p i d -> p (i d)"),
                                   ctx_raw[:, b * KEYS:(b + 1) * KEYS],
                                   ctx_hi[:, b].bitcast(F32).rearrange("p i d -> p (i d)"),
                                   ALU.subtract).then_inc(ctx_lo_ready, 1)
            for n in (1, 2):
                for b in range(B):
                    power(b, n)

        @block.tensor
        def _(pe):
            def ctx_chunk(c):
                b, k = divmod(c, NCH)
                pe.wait_ge(ld_ctx[c], 16)
                if c == 0:
                    pe.wait_ge(consts, 6)
                if c >= 4:
                    pe.wait_ge(ctxT_lo_ready, c - 3)
                for i in range(4):
                    blk = b * NBLK + 4 * k + i
                    last = pe.transpose(bank[c % 4][:, i * P:(i + 1) * P], ctx_raw[:, blk * P:(blk + 1) * P], ident[:])
                last.then_inc(ctxT_psum, 1)

            def xn_transpose(b, n, dst):
                pe.wait_ge(xn_ready, B * n + b + 1)
                for k in range(HB):
                    last = pe.transpose(dst[:, k * P:(k + 1) * P], xn[:, b, k * P:(k + 1) * P], ident[:])
                last.then_inc(xnT_psum, 1)

            def wk_transpose(g):
                pe.wait_ge(ld_wk, 16 * (g + 1))
                after(pe, qk_lo_ready, 2 * g)
                pe.transpose(WQK_BANK[:, 0:P], wk[:], ident[:]).then_inc(wkT_psum, 1)

            def q_project(g, j):
                if j == 0:
                    pe.wait_ge(ld_wq, 16 * (g + 1))
                for k in range(HB):
                    last = pe.matmul(QYO_BANK[:].rearrange("p (b j t) -> p j b t", b=B, j=J)[:, j],
                                     wq[:, k, j * P:(j + 1) * P], xnT[:, k, :].rearrange("p (b t) -> p b t", b=B),
                                     start=(k == 0), stop=(k == HB - 1))
                if j == J - 1:
                    last.then_inc(q_psum, 1)

            def q_fold(g):
                pe.wait_ge(wkT_ready, g + 1)
                pe.wait_ge(q_ready, g + 1)
                pe.matmul(WQK_BANK[:], wkT[:], qT[:].rearrange("p b j t -> p (b j t)"),
                          start=True, stop=True).then_inc(qk_psum, 1)

            def step(g, n, scores_on, trans_on, av_on, fold_on, out_on):
                N = STEPS * g + n
                if scores_on:
                    b, j, k = n // SPU, n % SPU // NCH, n % NCH
                    if n % SPU == 0:
                        pe.wait_ge(qk_hi_ready, 2 * g + b + 1)
                        pe.wait_ge(qk_lo_ready, 2 * g + b + 1)
                    after(pe, masked, N - 1)
                    keys = slice(k * CH, (k + 1) * CH)
                    pe.matmul(S_BANK[n % 2][:], qk_hi[:, b, j], ctxT_lo[:, b, keys], start=True, stop=False)
                    pe.matmul(S_BANK[n % 2][:], qk_lo[:, b, j], ctxT_hi[:, b, keys], start=False, stop=False)
                    pe.matmul(S_BANK[n % 2][:], qk_hi[:, b, j], ctxT_hi[:, b, keys],
                              start=False, stop=True).then_inc(scores, 1)
                if trans_on:
                    t = N - LAG_T
                    p, b = (n - LAG_T) % SPU, (n - LAG_T) // SPU % 2
                    if p in (0, SPU // 2):
                        pe.wait_ge(exps, 4 * (2 * g + (n - LAG_T) // SPU) + (3 if p == 0 else 4))
                    after(pe, pT_lo_ready, t - 1)
                    for i in range(2):
                        for j in range(J):
                            at = (i * J + j) * P
                            last = pe.transpose(PT_BANK[n % 2][:, at:at + P],
                                                probs[:, b, j, (2 * p + i) * P:(2 * p + i + 1) * P], ident[:])
                    last.then_inc(pT_psum, 1)
                if av_on:
                    a = N - LAG_A
                    p, b = (n - LAG_A) % SPU, (n - LAG_A) // SPU % 2
                    pe.wait_ge(pT_lo_ready, a + 1)
                    s = (n - LAG_A) % PTR
                    for i in range(2):
                        blk, cols = 2 * p + i, slice(i * J * P, (i + 1) * J * P)
                        dst = O_BANK[b][:, 0:J * T]
                        pe.matmul(dst, ctx_lo[:, b, blk], pT_hi[:, s, cols], start=(blk == 0), stop=False)
                        pe.matmul(dst, ctx_hi[:, b, blk], pT_lo[:, s, cols], start=False, stop=False)
                        last = pe.matmul(dst, ctx_hi[:, b, blk], pT_hi[:, s, cols], start=False, stop=(blk == NBLK - 1))
                    last.then_inc(av, 1)
                if out_on and n in (4, 12):
                    u = 2 * (g - 1) + n // SPU
                    if n == 4:
                        pe.wait_ge(ld_wv, 16 * g)
                    pe.wait_ge(oT_ready, u + 1)
                    if not scores_on:
                        pe.wait_ge(added, 2 * u)
                    if n == 12 and fold_on:
                        pe.wait_ge(q_ready, g + 2)
                    pe.matmul(QYO_BANK[:, 0:J * T], wv[:], oT[:], start=True, stop=True).then_inc(y_psum, 1)
                if out_on and n in (6, 14):
                    u = 2 * (g - 1) + n // SPU
                    if n == 6:
                        pe.wait_ge(ld_wo, 16 * g)
                    pe.wait_ge(yT_ready, u + 1)
                    for j in range(J):
                        last = pe.matmul(QYO_BANK[:, j * H:(j + 1) * H], yT[:, j], wo[:, j], start=True, stop=True)
                    last.then_inc(out_psum, 1)
                if fold_on and n == 9:
                    wk_transpose(g + 1)
                    after(pe, added, 2 * (2 * g - 1))
                    q_project(g + 1, 0)
                if fold_on and n == 10:
                    q_project(g + 1, 1)
                if fold_on and n == 12:
                    q_fold(g + 1)

            for c in range(4):
                ctx_chunk(c)
            for b in range(B):
                xn_transpose(b, 0, O_BANK[b])
            wk_transpose(0)
            pe.wait_ge(xnT_ready, 2)
            q_project(0, 0)
            q_project(0, 1)
            for c in (4, 5):
                ctx_chunk(c)
            q_fold(0)
            for c in (6, 7):
                ctx_chunk(c)
            pe.wait_ge(ctxT_lo_ready, B * NCH)

            for n in range(STEPS):
                if n == LAG_A:
                    pe.wait_ge(ctx_lo_ready, B)
                step(0, n, True, n >= LAG_T, n >= LAG_A, True, False)
            with pe.Fori(1, G - 1) as g:
                for n in range(STEPS):
                    step(g, n, True, True, True, True, True)
            for n in range(STEPS):
                step(G - 1, n, True, True, True, False, True)
            for n in range(STEPS):
                step(G, n, False, n < LAG_T, n < LAG_A, False, True)

            QA, QB, KV = bank[0], bank[1], bank[2]
            SC, PT2, DN = bank[3:5], bank[5:7], [bank[7], bank[0]]

            def project2(r):
                for half, (dst, done) in enumerate(((QA, qa_psum), (QB, qb_psum))):
                    if half == 0:
                        pe.wait_ge(ld_wq2, 16 * (r + 1))
                        after(pe, added2, 2 * r - 2)
                    for h in range(2):
                        for k in range(HB):
                            last = pe.matmul(dst[:, h * B * T:(h + 1) * B * T],
                                             wq2[:, k, (2 * half + h) * P:(2 * half + h + 1) * P], xnT[:, k, :],
                                             start=(k == 0), stop=(k == HB - 1))
                    last.then_inc(done, 1)
                pe.wait_ge(ld_wk2, 16 * (r + 1))
                after(pe, v2_ready, r)
                for k in range(HB):
                    last = pe.matmul(KV[:, 0:B * T], wkv2[:, k, 0, :], xnT[:, k, :], start=(k == 0), stop=(k == HB - 1))
                last.then_inc(k2_psum, 1)
                pe.wait_ge(ld_wv2, 16 * (r + 1))
                for b in range(B):
                    for k in range(HB):
                        last = pe.matmul(KV[:, (B + b) * P:(B + b + 1) * P], xnT[:, k, b * T:(b + 1) * T],
                                         wkv2[:, k, 1, :], start=(k == 0), stop=(k == HB - 1))
                last.then_inc(v2_psum, 1)

            def group2(r, first, last_group):
                pe.wait_ge(qa_ready, r + 1)
                pe.wait_ge(qb_ready, r + 1)
                pe.wait_ge(k2_ready, r + 1)
                for b in range(B):
                    after(pe, c2_ready, 2 * (r - 1) + b + 1)
                    for h in range(HR):
                        mm = pe.matmul(SC[b][:, h * P:(h + 1) * P], q2T[:, h, b * T:(b + 1) * T],
                                       k2T[:, b * T:(b + 1) * T], start=True, stop=True)
                    mm.then_inc(s2_psum, 1)
                if not last_group:
                    project2(r + 1)
                for b in range(B):
                    pe.wait_ge(s2_probs, 2 * r + b + 1)
                    after(pe, p2T_ready, 2 * (r - 1) + b + 1)
                    for h in range(HR):
                        mm = pe.transpose(PT2[b][:, h * P:(h + 1) * P], p2[:, b, h], ident[:])
                    mm.then_inc(p2T_psum, 1)
                pe.wait_ge(v2_ready, r + 1)
                for b in range(B):
                    pe.wait_ge(p2T_ready, 2 * r + b + 1)
                    pe.matmul(SC[b][:], v2[:, b], p2T[:, b], start=True, stop=True).then_inc(c2_psum, 1)
                pe.wait_ge(ld_wd2, 16 * (r + 1))
                for b in range(B):
                    pe.wait_ge(c2_ready, 2 * r + b + 1)
                    after(pe, added2, 2 * (r - 1) + b + 1)
                    if b == 1 and not last_group:
                        pe.wait_ge(qa_ready, r + 2)
                    for h in range(HR):
                        mm = pe.matmul(DN[b][:, 0:H], c2T[:, b, h * P:(h + 1) * P], wd2[:, h, :],
                                       start=(h == 0), stop=(h == HR - 1))
                    mm.then_inc(d2_psum, 1)

            for b in range(B):
                xn_transpose(b, 1, PT_BANK[b])
            pe.wait_ge(xnT_ready, 2 * B)
            project2(0)
            group2(0, True, False)
            with pe.Fori(1, R - 1) as r:
                group2(r, False, False)
            group2(R - 1, False, True)

            GU, DWN = bank[0:2], bank[3:5]
            for b in range(B):
                xn_transpose(b, 2, (bank[2], bank[5])[b])
            pe.wait_ge(xnT_ready, 3 * B)
            pe.wait_ge(ld_gate, 32)
            for b in range(B):
                for k in range(HB):
                    mm = pe.matmul(bank[6][:, b * E:(b + 1) * E], xnT[:, k, b * T:(b + 1) * T], gatew[:, k, :],
                                   start=(k == 0), stop=(k == HB - 1))
            mm.then_inc(logits, 1)

            def gate_up(i, s, loads):
                m = RING * i + s
                pe.wait_ge(ld_ring[s], loads)
                after(pe, h_ready, m - 1)
                for half in range(2):
                    for k in range(HB):
                        mm = pe.matmul(GU[s % 2][:, half * B * T:(half + 1) * B * T],
                                       ring_gu[:, s, k, half * F:(half + 1) * F], xnT[:, k, :],
                                       start=(k == 0), stop=(k == HB - 1))
                mm.then_inc(gu_psum, 1)

            def down(i, s):
                m = RING * i + s
                pe.wait_ge(h_ready, m + 1)
                after(pe, added3, B * (m - 1))
                for b in range(B):
                    mm = pe.matmul(DWN[s % 2][:, b * H:(b + 1) * H], hT[:, s % 2, b * T:(b + 1) * T],
                                   ring_dn[:, s, :], start=True, stop=True)
                mm.then_inc(down_psum, 1)

            def loads_before(i, s):
                return (48 if s == 0 else 32) + 32 * i

            gate_up(0, 0, loads_before(0, 0))
            for s in range(1, RING):
                gate_up(0, s, loads_before(0, s))
                down(0, s - 1)
            with pe.Fori(1, E // RING) as i:
                for s in range(RING):
                    gate_up(i, s, loads_before(i, s))
                    if s == 0:
                        down(i - 1, RING - 1)
                    else:
                        down(i, s - 1)
            gate_up(E // RING, 0, loads_before(E // RING, 0))
            down(E // RING - 1, RING - 1)
            down(E // RING, 0)

        @block.scalar
        def _(act):
            for c in range(B * NCH):
                b, k = divmod(c, NCH)
                act.dma_start(ctx_raw[:, c * CH:(c + 1) * CH], ctx_v[b, :, k * CH:(k + 1) * CH]).then_inc(ld_ctx[c], 16)

            def ctx_chunk(c):
                b, k = divmod(c, NCH)
                act.wait_ge(ctxT_psum, c + 1)
                act.activation(ctxT_hi[:, b, k * CH:(k + 1) * CH], bank[c % 4][:], ACT.Copy).then_inc(ctxT_hi_ready, 1)

            def xnT_copy(b, n, src):
                act.wait_ge(xnT_psum, B * n + b + 1)
                act.activation(xnT[:, :, b * T:(b + 1) * T], src[:, 0:HB * P].rearrange("p (k t) -> p k t", k=HB),
                               ACT.Copy).then_inc(xnT_ready, 1)

            def wkT_copy(g):
                act.wait_ge(wkT_psum, g + 1)
                act.activation(wkT[:], WQK_BANK[:, 0:P], ACT.Copy).then_inc(wkT_ready, 1)

            def q_copy(g):
                act.wait_ge(q_psum, g + 1)
                act.activation(qT[:].rearrange("p b j t -> p (b j t)"), QYO_BANK[:], ACT.Copy).then_inc(q_ready, 1)

            def fold_copy(g, b):
                if b == 0:
                    act.wait_ge(qk_psum, g + 1)
                else:
                    act.wait_ge(qk_lo_ready, 2 * g + 1)
                after(act, scores, STEPS * (g - 1) + SPU * (b + 1))
                act.activation(qk_hi[:, b].rearrange("p j t -> p (j t)"), WQK_BANK[:, b * J * T:(b + 1) * J * T],
                               ACT.Copy).then_inc(qk_hi_ready, 1)

            def exp_half(g, du, j, half):
                u = 2 * g + du
                b = du % 2
                if half == 0:
                    act.wait_ge(negmax_ready, 2 * u + j + 1)
                part = probs[:, b, j, half * (KEYS // 2):(half + 1) * (KEYS // 2)]
                act.activation(part, part, ACT.Exp, bias=negmax[:, b, j:j + 1], scale=SCALE,
                               accum_out=den[:, b, j, half:half + 1]).then_inc(exps, 1)

            EXPS = {1: (-1, 1, 0), 3: (-1, 1, 1), 5: (0, 0, 0), 7: (0, 0, 1),
                    9: (0, 1, 0), 11: (0, 1, 1), 13: (1, 0, 0), 15: (1, 0, 1)}

            def step(g, n, exp_on, trans_on, fold_on, fold2_on, out_on):
                t = STEPS * g + n - LAG_T
                if out_on and n in (4, 12):
                    u = 2 * (g - 1) + n // SPU
                    act.wait_ge(av, SPU * (u + 1))
                    act.activation(oT[:], O_BANK[n // SPU][:, 0:J * T], ACT.Copy).then_inc(oT_ready, 1)
                if exp_on and n in EXPS:
                    exp_half(g, *EXPS[n])
                if trans_on:
                    after(act, av, t - PTR + 1)
                    act.wait_ge(pT_psum, t + 1)
                    act.activation(pT_hi[:, (n - LAG_T) % PTR], PT_BANK[n % 2][:], ACT.Copy).then_inc(pT_hi_ready, 1)
                if fold2_on and n == 0:
                    fold_copy(g, 1)
                if out_on and n in (5, 13):
                    u = 2 * (g - 1) + n // SPU
                    act.wait_ge(y_psum, u + 1)
                    act.activation(yT[:].rearrange("p j t -> p (j t)"), QYO_BANK[:, 0:J * T],
                                   ACT.Copy).then_inc(yT_ready, 1)
                if fold_on and n == 10:
                    wkT_copy(g + 1)
                if fold_on and n == 11:
                    q_copy(g + 1)
                if fold_on and n == 13:
                    fold_copy(g + 1, 0)

            for c in range(4):
                ctx_chunk(c)
            for b in range(B):
                xnT_copy(b, 0, O_BANK[b])
            wkT_copy(0)
            q_copy(0)
            for c in (4, 5):
                ctx_chunk(c)
            fold_copy(0, 0)
            for c in (6, 7):
                ctx_chunk(c)

            for n in range(STEPS):
                step(0, n, n >= 5, n >= LAG_T, True, True, False)
            with act.Fori(1, G - 1) as g:
                for n in range(STEPS):
                    step(g, n, True, True, True, True, True)
            for n in range(STEPS):
                step(G - 1, n, True, True, False, True, True)
            for n in range(STEPS):
                step(G, n, n < 5, n < LAG_T, False, False, True)

            QA, QB, KV = bank[0], bank[1], bank[2]
            SC, PT2 = bank[3:5], bank[5:7]

            def copy_qk(r):
                after(act, s2_psum, 2 * r)
                act.wait_ge(qa_psum, r + 1)
                act.activation(q2T[:, 0:2].rearrange("p h t -> p (h t)"), QA[:], ACT.Copy).then_inc(qa_ready, 1)
                act.wait_ge(v2_psum, r + 1)
                act.activation(k2T, KV[:, 0:B * T], ACT.Copy).then_inc(k2_ready, 1)

            def group2(r, last_group):
                for b in range(B):
                    act.wait_ge(s2_negmax, 2 * r + b + 1)
                    for h in range(HR):
                        act.activation(p2[:, b, h], p2[:, b, h], ACT.Exp, bias=nm2[:, b, h:h + 1],
                                       accum_out=ds2[:, b, h:h + 1]).then_inc(s2_exps, 1)
                    if b == 0 and not last_group:
                        copy_qk(r + 1)
                for b in range(B):
                    after(act, c2_psum, 2 * (r - 1) + b + 1)
                    act.wait_ge(p2T_psum, 2 * r + b + 1)
                    act.activation(p2T[:, b], PT2[b][:], ACT.Copy).then_inc(p2T_ready, 1)
                for b in range(B):
                    after(act, d2_psum, 2 * (r - 1) + b + 1)
                    act.wait_ge(c2_psum, 2 * r + b + 1)
                    act.activation(c2T[:, b], SC[b][:], ACT.Copy).then_inc(c2_ready, 1)

            for b in range(B):
                xnT_copy(b, 1, PT_BANK[b])
            copy_qk(0)
            group2(0, False)
            with act.Fori(1, R - 1) as r:
                group2(r, False)
            group2(R - 1, True)

            GU = bank[0:2]
            for b in range(B):
                xnT_copy(b, 2, (bank[2], bank[5])[b])
            act.wait_ge(logits, 1)
            act.activation(route[:, 0].rearrange("p b e -> p (b e)"), bank[6][:, 0:B * E], ACT.Exp,
                           scale=-1.0).then_inc(gate_exp, 1)

            def silu(m, s):
                after(act, h_ready, m - 1)
                act.wait_ge(gu_psum, m + 1)
                act.activation(sg[:, s % 2], GU[s % 2][:, 0:B * T], ACT.Silu).then_inc(silu_ready, 1)

            for s in range(RING):
                silu(s, s)
            with act.Fori(1, E // RING) as i:
                for s in range(RING):
                    silu(RING * i + s, s)
            silu(E, 0)

        @block.vector
        def _(dve):
            def norm_stats(b, n):
                o = 3 * (B * n + b)
                dve.bn_stats(stats[:, b, :], resid[:, b, :]).then_inc(ln_stat, 1)
                dve.wait_ge(ln_stat, o + 1)
                dve.bn_aggr(meanvar[:, b, :], stats[:, b, :]).then_inc(ln_stat, 1)
                dve.wait_ge(ln_stat, o + 2)
                dve.tensor_scalar(var_eps[:, b], meanvar[:, b, 1:2], EPS, None, ALU.add).then_inc(ln_stat, 1)

            def norm_apply(b, n):
                dve.wait_ge(ln_pow, B * n + b + 1)
                after(dve, xnT_psum, B * (n - 1) + b + 1)
                dve.tensor_scalar(xn[:, b, :], resid[:, b, :], meanvar[:, b, 0:1], rstd[:, b],
                                  ALU.subtract, ALU.mult).then_inc(xn_ready, 1)

            def ctx_chunk(c):
                b, k = divmod(c, NCH)
                dve.wait_ge(ctxT_hi_ready, c + 1)
                cols = slice(k * CH, (k + 1) * CH)
                dve.tensor_tensor(ctxT_lo[:, b, cols], bank[c % 4][:], ctxT_hi[:, b, cols].bitcast(F32),
                                  ALU.subtract).then_inc(ctxT_lo_ready, 1)

            def ctx_round(b):
                for k in range(NCH):
                    dve.wait_ge(ld_ctx[b * NCH + k], 16)
                dve.tensor_copy(ctx_hi[:, b].rearrange("p i d -> p (i d)"),
                                ctx_raw[:, b * KEYS:(b + 1) * KEYS]).then_inc(ctx_hi_ready, 1)

            def fold_rest(g, b):
                dve.wait_ge(qk_hi_ready, 2 * g + b + 1)
                dve.tensor_tensor(qk_lo[:, b].rearrange("p j t -> p (j t)"), WQK_BANK[:, b * J * T:(b + 1) * J * T],
                                  qk_hi[:, b].bitcast(F32).rearrange("p j t -> p (j t)"),
                                  ALU.subtract).then_inc(qk_lo_ready, 1)

            def denominators(g, du):
                u, b = 2 * g + du, du % 2
                dve.wait_ge(exps, 4 * u + 4)
                dve.tensor_tensor(dsum[:, b], den[:, b, :, 0], den[:, b, :, 1], ALU.add).then_inc(rden_step, 1)
                dve.wait_ge(rden_step, 3 * u + 1)
                dve.reciprocal(dsum[:, b], dsum[:, b]).then_inc(rden_step, 1)
                dve.wait_ge(rden_step, 3 * u + 2)
                dve.scalar_tensor_tensor(rden[:, b], rmax[:, b, :, NCH - 1], NEG / 2, dsum[:, b],
                                         ALU.is_gt, ALU.mult).then_inc(rden_step, 1)

            def step(g, n, scores_on, trans_on, fold_on, fold2_on, rden_on, out_on):
                N = STEPS * g + n
                t = N - LAG_T
                if scores_on:
                    b, j, k = n // SPU, n % SPU // NCH, n % NCH
                    dve.wait_ge(scores, N + 1)
                    after(dve, masked, N)
                if trans_on:
                    dve.wait_ge(pT_hi_ready, t + 1)
                    dve.tensor_tensor(pT_lo[:, (n - LAG_T) % PTR], PT_BANK[n % 2][:],
                                      pT_hi[:, (n - LAG_T) % PTR].bitcast(F32), ALU.subtract).then_inc(pT_lo_ready, 1)
                if scores_on:
                    keys = slice(k * CH, (k + 1) * CH)
                    dve.tensor_tensor_reduce(out=probs[:, b, j, keys], in0=S_BANK[n % 2][:], in1=mask_bias[:, b, keys],
                                             scale=1.0, scalar=(NEG if k == 0 else rmax[:, b, j, k - 1:k]),
                                             op0=ALU.add, op1=ALU.max,
                                             accum_out=rmax[:, b, j, k:k + 1]).then_inc(masked, 1)
                    if k == NCH - 1:
                        dve.wait_ge(masked, N + 1)
                        dve.tensor_scalar(negmax[:, b, j:j + 1], rmax[:, b, j, k:k + 1], -SCALE, None,
                                          ALU.mult).then_inc(negmax_ready, 1)
                if rden_on and n == 5:
                    denominators(g, -1)
                if rden_on and n == 13:
                    denominators(g, 0)
                if fold2_on and n == 1:
                    fold_rest(g, 1)
                if fold_on and n == 14:
                    fold_rest(g + 1, 0)
                if out_on and n in (7, 15):
                    b = n // SPU
                    u = 2 * (g - 1) + b
                    dve.wait_ge(out_psum, u + 1)
                    for j in range(J):
                        if j:
                            dve.wait_ge(added, 2 * u + 1)
                        dve.scalar_tensor_tensor(resid[:, b, :], QYO_BANK[:, j * H:(j + 1) * H], rden[:, b, j:j + 1],
                                                 resid[:, b, :], ALU.mult, ALU.add).then_inc(added, 1)

            dve.wait_ge(ld_x, 16)
            norm_stats(0, 0)
            norm_stats(1, 0)
            norm_apply(0, 0)
            norm_apply(1, 0)
            for c in range(4):
                ctx_chunk(c)
            ctx_round(0)
            for c in (4, 5):
                ctx_chunk(c)
            fold_rest(0, 0)
            for c in (6, 7):
                ctx_chunk(c)
            ctx_round(1)
            dve.wait_ge(mask_ready, B)

            for n in range(STEPS):
                step(0, n, True, n >= LAG_T, True, True, n == 13, False)
            with dve.Fori(1, G - 1) as g:
                for n in range(STEPS):
                    step(g, n, True, True, True, True, True, True)
            for n in range(STEPS):
                step(G - 1, n, True, True, False, True, True, True)
            for n in range(STEPS):
                step(G, n, False, n < LAG_T, False, False, n == 5, True)
                if n in (7, 15):
                    b = n // SPU
                    dve.wait_ge(added, 2 * (2 * (G - 1) + b + 1))
                    norm_stats(b, 1)
                    norm_apply(b, 1)

            QB, KV = bank[1], bank[2]
            SC, DN = bank[3:5], [bank[7], bank[0]]

            def copy_qb(r):
                after(dve, s2_psum, 2 * r)
                dve.wait_ge(qb_psum, r + 1)
                dve.tensor_copy(q2T[:, 2:4].rearrange("p h t -> p (h t)"), QB[:]).then_inc(qb_ready, 1)

            def copy_v(r):
                after(dve, c2_psum, 2 * r)
                dve.wait_ge(k2_ready, r + 1)
                dve.wait_ge(v2_psum, r + 1)
                dve.tensor_copy(v2.rearrange("p b d -> p (b d)"), KV[:, B * P:2 * B * P]).then_inc(v2_ready, 1)

            def group2(r, last_group):
                for b in range(B):
                    dve.wait_ge(s2_psum, 2 * r + b + 1)
                    after(dve, p2T_psum, 2 * (r - 1) + b + 1)
                    dve.scalar_tensor_tensor(p2[:, b], SC[b][:].rearrange("p (h k) -> p h k", h=HR), SCALE,
                                             causal[:].unsqueeze(1).broadcast_to([P, HR, P]),
                                             ALU.mult, ALU.add).then_inc(s2_masked, 1)
                    dve.wait_ge(s2_masked, 2 * r + b + 1)
                    dve.tensor_reduce(nm2[:, b], p2[:, b], AX.X, ALU.max, negate=True).then_inc(s2_negmax, 1)
                if not last_group:
                    copy_qb(r + 1)
                for b in range(B):
                    dve.wait_ge(s2_exps, HR * (2 * r + b + 1))
                    dve.reciprocal(rd2[:, b], ds2[:, b]).then_inc(s2_rden, 1)
                    dve.wait_ge(s2_rden, 2 * r + b + 1)
                    dve.tensor_tensor(p2[:, b], p2[:, b], rd2[:, b].unsqueeze(2).broadcast_to([P, HR, P]),
                                      ALU.mult).then_inc(s2_probs, 1)
                for b in range(B):
                    dve.wait_ge(d2_psum, 2 * r + b + 1)
                    dve.tensor_tensor(resid[:, b, :], DN[b][:, 0:H], resid[:, b, :], ALU.add).then_inc(added2, 1)
                if not last_group:
                    copy_v(r + 1)

            copy_qb(0)
            copy_v(0)
            group2(0, False)
            with dve.Fori(1, R - 1) as r:
                group2(r, False)
            group2(R - 1, True)

            GU, DWN = bank[0:2], bank[3:5]
            for b in range(B):
                dve.wait_ge(added2, 2 * (R - 1) + b + 1)
                norm_stats(b, 2)
            for b in range(B):
                norm_apply(b, 2)

            ex, sc, biased, eq, cand, hot1, hot2, comb = (route[:, i] for i in range(8))
            top1, at1, top2, at2, total, rtotal = (r1[:, i] for i in range(6))

            def wide(v):
                return v.broadcast_to([P, B, E])

            flow = [0]

            def chained(ins):
                flow[0] += 1
                ins.then_inc(route_step, 1)
                dve.wait_ge(route_step, flow[0])

            def router():
                dve.wait_ge(gate_exp, 1)
                dve.wait_ge(ld_gate, 32)
                chained(dve.tensor_scalar(sc, ex, 1.0, None, ALU.add))
                chained(dve.reciprocal(sc, sc))
                chained(dve.tensor_tensor(biased, sc, bias_b[:].broadcast_to([P, B, E]), ALU.add))
                for top, at, hot in ((top1, at1, hot1), (top2, at2, hot2)):
                    chained(dve.tensor_reduce(top, biased, AX.X, ALU.max))
                    chained(dve.tensor_tensor(eq, biased, wide(top), ALU.is_equal))
                    chained(dve.tensor_tensor(cand, eq, rank[:].broadcast_to([P, B, E]), ALU.mult))
                    chained(dve.tensor_reduce(at, cand, AX.X, ALU.max))
                    chained(dve.tensor_tensor(hot, cand, wide(at), ALU.is_equal))
                    if hot is hot1:
                        chained(dve.scalar_tensor_tensor(biased, hot1, NEG, biased, ALU.mult, ALU.add))
                chained(dve.tensor_tensor(hot1, hot1, hot2, ALU.add))
                chained(dve.tensor_tensor(comb, hot1, sc, ALU.mult))
                chained(dve.tensor_reduce(total, comb, AX.X, ALU.add))
                chained(dve.tensor_scalar(total, total, 1e-20, None, ALU.add))
                chained(dve.reciprocal(rtotal, total))
                chained(dve.tensor_tensor(comb, comb, wide(rtotal), ALU.mult))

            def gated(m, s):
                after(dve, down_psum, m - 1)
                dve.wait_ge(silu_ready, m + 1)
                dve.tensor_tensor(hT[:, s % 2], GU[s % 2][:, B * T:2 * B * T], sg[:, s % 2],
                                  ALU.mult).then_inc(h_ready, 1)

            def add_expert(m, s):
                dve.wait_ge(down_psum, m + 1)
                for b in range(B):
                    dve.wait_ge(added3, B * (m - 1) + b + 1)
                    dve.scalar_tensor_tensor(resid[:, b, :], DWN[s % 2][:, b * H:(b + 1) * H],
                                             comb[:, b, bass.ds(m - 1, 1)], resid[:, b, :],
                                             ALU.mult, ALU.add).then_inc(added3, 1)

            router()
            gated(0, 0)
            gated(1, 1)
            dve.wait_ge(down_psum, 1)
            for b in range(B):
                dve.tensor_tensor(resid[:, b, :], DWN[0][:, b * H:(b + 1) * H], resid[:, b, :],
                                  ALU.add).then_inc(added3, 1)
            for s in range(2, RING):
                gated(s, s)
                add_expert(s - 1, s - 1)
            with dve.Fori(1, E // RING) as i:
                for s in range(RING):
                    gated(RING * i + s, s)
                    add_expert(RING * i + s - 1, (s - 1) % RING)
            gated(E, 0)
            add_expert(E - 1, RING - 1)
            add_expert(E, 0)


_INS = ['x', 'ctx_1024', 'mask_BxS2_bf1', 'L0_xattn_Wq', 'L0_xattn_Wk', 'L0_xattn_Wv', 'L0_xattn_Wo',
        'L0_attn_w_q', 'L0_attn_w_kv', 'L0_attn_w_dense', 'L0_ffn_gate_w', 'L0_ffn_expert_bias',
        'L0_ffn_shared_gate_w', 'L0_ffn_shared_up_w', 'L0_ffn_shared_down_w', 'L0_ffn_experts_gate_up',
        'L0_ffn_experts_down']
_OUTS = [((2, 128, 256), 'float32')]


def kernel(**inputs):
    import numpy as _np
    import concourse.bacc as _bacc
    from concourse import mybir as _mybir
    from concourse.bass_utils import run_bass_kernel_spmd as _run

    nc = _bacc.Bacc("TRN2", target_bir_lowering=False, num_devices=1)
    arrays, args = {}, []
    for name in _INS:
        a = _np.ascontiguousarray(inputs[name])
        arrays[f"in_{name}_dram"] = a
        args.append(nc.dram_tensor(f"in_{name}_dram", a.shape, _mybir.dt.from_np(a.dtype), kind="ExternalInput").ap())
    for i, (shape, dtype) in enumerate(_OUTS):
        dt = _mybir.dt.from_np(_np.dtype(dtype))
        args.append(nc.dram_tensor(f"out_{i}_dram", shape, dt, kind="ExternalOutput").ap())
    perceiver_layer(nc, *args)
    r = _run(nc, [arrays], core_ids=[0])
    got = tuple(r.results[0][f"out_{i}_dram"] for i in range(len(_OUTS)))
    return got[0]
```

```python
from contextlib import ExitStack

import concourse.bass as bass
from concourse import mybir

ALU = mybir.AluOpType
ACT = mybir.ActivationFunctionType
AX = mybir.AxisListType
F32 = mybir.dt.float32
F32R = mybir.dt.float32r
U8 = mybir.dt.uint8

P = 128
NEG = -1e38
EPS = 1e-5


def after(eng, sem, value):
    if not isinstance(value, int) or value > 0:
        eng.wait_ge(sem, value)


def perceiver_layer(nc, x, ctx_tokens, key_mask, xq_w, xk_w, xv_w, xo_w, sq_w, skv_w, sd_w,
                    gate_w, expert_bias, sh_gate_w, sh_up_w, sh_down_w, ex_gu_w, ex_down_w, out):
    B, T, H = x.shape
    _, KEYS, VIS = ctx_tokens.shape
    assert B == 2 and T == P and VIS == P and H == 2 * P
    HB = H // P
    XH = xq_w.shape[1] // P
    G = xk_w.shape[1] // P
    J = XH // G
    NBLK = KEYS // P
    CH = 512
    NCH = KEYS // CH
    SCALE = float(P) ** -0.5
    SH = sq_w.shape[1] // P
    R = skv_w.shape[1] // (2 * P)
    HR = SH // R
    E = gate_w.shape[1]
    F = ex_down_w.shape[1]
    RING = 4
    assert J == 2 and NCH == 4 and HR == 4 and F == P and E % RING == 0

    SPU = J * NCH
    STEPS = 2 * SPU
    LAG_T = SPU + 2
    LAG_A = LAG_T + 2
    NT = G * STEPS
    PTR = 4

    xq_v = xq_w.rearrange("(k p) (g e) -> g p k e", p=P, g=G)
    xk_v = xk_w.rearrange("p (g e) -> g p e", g=G)
    xv_v = xv_w.rearrange("p (g e) -> g p e", g=G)
    xo_v = xo_w.rearrange("(g j p) n -> g p j n", p=P, g=G)
    sq_v = sq_w.rearrange("(k p) (r e) -> r p k e", p=P, r=R)
    skv_v = skv_w.rearrange("(k p) (s r e) -> r s p k e", p=P, s=2, r=R)
    sd_v = sd_w.rearrange("(r h p) n -> r p h n", p=P, r=R)
    exgu_v = ex_gu_w.rearrange("e (k p) f -> e p k f", p=P)
    x_v = x.rearrange("b t d -> t b d")
    out_v = out.rearrange("b t d -> t b d")
    ctx_v = ctx_tokens.rearrange("b (p i) d -> b p (i d)", p=P)

    with ExitStack() as stack:
        def sb(name, shape, dt=F32):
            return stack.enter_context(nc.sbuf_tensor(name, shape, dt))

        def sem(name):
            return stack.enter_context(nc.semaphore(name))

        resid = sb("resid", [P, B, H])
        xn = sb("xn", [P, B, H])
        xnT_hi = sb("xnT_hi", [P, HB, B * T], F32R)
        xnT_lo = sb("xnT_lo", [P, HB, B * T], F32R)
        xnT = sb("xnT", [P, HB, B * T])
        ones = sb("ones", [P, CH])
        ident = sb("ident", [P, P])
        causal = sb("causal", [P, P])
        minus_half = sb("minus_half", [P, 1])
        ctx_raw = sb("ctx_raw", [P, B * KEYS])
        ctx_hi = sb("ctx_hi", [P, B, NBLK, P], F32R)
        ctx_lo = sb("ctx_lo", [P, B, NBLK, P], F32R)
        ctxT_hi = sb("ctxT_hi", [P, B, KEYS], F32R)
        ctxT_lo = sb("ctxT_lo", [P, B, KEYS], F32R)
        mask8 = sb("mask8", [P, B, KEYS], U8)
        mask_bias = sb("mask_bias", [P, B, KEYS])
        probs = sb("probs", [P, B, J, KEYS])
        pT_hi = sb("pT_hi", [P, PTR, CH], F32R)
        pT_lo = sb("pT_lo", [P, PTR, CH], F32R)
        wq = sb("wq", [P, HB, J * P])
        wq_hi = sb("wq_hi", [P, HB, J * P], F32R)
        wq_lo = sb("wq_lo", [P, HB, J * P], F32R)
        wk = sb("wk", [P, P])
        wv = sb("wv", [P, P])
        wo = sb("wo", [P, J, H])
        wv_hi, wv_lo = sb("wv_hi", [P, P], F32R), sb("wv_lo", [P, P], F32R)
        wo_hi, wo_lo = sb("wo_hi", [P, J, H], F32R), sb("wo_lo", [P, J, H], F32R)
        wkT_hi, wkT_lo = sb("wkT_hi", [P, P], F32R), sb("wkT_lo", [P, P], F32R)
        qT_hi, qT_lo = sb("qT_hi", [P, B * J * T], F32R), sb("qT_lo", [P, B * J * T], F32R)
        qk_hi = sb("qk_hi", [P, B, J, T], F32R)
        qk_lo = sb("qk_lo", [P, B, J, T], F32R)
        oT_hi, oT_lo = sb("oT_hi", [P, J * T], F32R), sb("oT_lo", [P, J * T], F32R)
        yT_hi, yT_lo = sb("yT_hi", [P, J * T], F32R), sb("yT_lo", [P, J * T], F32R)
        stats = sb("stats", [P, B, 6])
        meanvar = sb("meanvar", [P, B, 2])
        var_eps = sb("var_eps", [P, B, 1])
        rstd = sb("rstd", [P, B, 1])
        rmax = sb("rmax", [P, B, J, NCH])
        negmax = sb("negmax", [P, B, J])
        den = sb("den", [P, B, J, 2])
        dsum = sb("dsum", [P, B, J])
        rden = sb("rden", [P, B, J])
        ring_gu = sb("ring_gu", [P, RING, HB, 2 * F])
        ring_dn = sb("ring_dn", [P, RING, H])
        gatew = sb("gatew", [P, HB, E])
        gatew_hi = sb("gatew_hi", [P, HB, E], F32R)
        gatew_lo = sb("gatew_lo", [P, HB, E], F32R)
        bias_b = sb("bias_b", [P, 1, E])
        rank = sb("rank", [P, 1, E])
        route = sb("route", [P, 10, B, E])
        r1 = sb("r1", [P, 6, B, 1])
        sc = route[:, 0]

        wq2 = ctx_raw[:, 0:1024]
        wkv2 = ctx_raw[:, 1024:1536]
        wd2 = ctx_raw[:, 1536:2560]
        parts_hi = ctxT_hi[:].rearrange("p b k -> p (b k)")
        parts_lo = ctxT_lo[:].rearrange("p b k -> p (b k)")
        wq2_hi, wq2_lo = parts_hi[:, 0:1024], parts_lo[:, 0:1024]
        wk2_hi, wk2_lo = (v[:, 1024:1280].rearrange("p (k e) -> p k e", k=HB) for v in (parts_hi, parts_lo))
        wk2 = wkv2.rearrange("p (k s e) -> p k s e", k=HB, s=2)[:, :, 0, :]
        wv2_raw = wkv2.rearrange("p (k s e) -> p k s e", k=HB, s=2)[:, :, 1, :]
        wv2 = ctx_raw[:, 2560:2816].rearrange("p (k e) -> p k e", k=HB)
        wd2_hi, wd2_lo = parts_hi[:, 1536:2560], parts_lo[:, 1536:2560]
        c2_hi = parts_hi[:, 2560:3584].rearrange("p (b n) -> p b n", b=B)
        c2_lo = parts_lo[:, 2560:3584].rearrange("p (b n) -> p b n", b=B)
        gu_hi, gu_lo = (
            v[:].rearrange("p b i d -> p (b i d)")[:, 0:RING * HB * 2 * F].rearrange("p (s n) -> p s n", s=RING)
            for v in (ctx_hi, ctx_lo))
        work = probs[:].rearrange("p b j k -> p (b j k)")
        q2T = work[:, 0:1024].rearrange("p (h t) -> p h t", h=HR)
        k2T = work[:, 1024:1280]
        v2 = work[:, 1280:1536].rearrange("p (b d) -> p b d", b=B)
        p2 = work[:, 1536:2560].rearrange("p (b h k) -> p b h k", b=B, h=HR)
        p2T = work[:, 2560:3584].rearrange("p (b n) -> p b n", b=B)
        nm2 = work[:, 4608:4616].rearrange("p (b h) -> p b h", b=B)
        ds2 = work[:, 4624:4632].rearrange("p (b h) -> p b h", b=B)
        rd2 = work[:, 4640:4648].rearrange("p (b h) -> p b h", b=B)
        sg = work[:, 5120:5632].rearrange("p (s t) -> p s t", s=2)
        hT = work[:, 5632:6144].rearrange("p (s t) -> p s t", s=2)

        bank = [stack.enter_context(nc.psum_tensor(f"bank{i}", [P, CH], F32)) for i in range(8)]
        S_BANK, PT_BANK, O_BANK = bank[0:2], bank[2:4], bank[4:6]
        WQK_BANK, QYO_BANK = bank[6], bank[7]

        ld_x = sem("ld_x")
        ld_ctx = [sem(f"ld_ctx{i}") for i in range(B * NCH)]
        ld_mask = [sem(f"ld_mask{b}") for b in range(B)]
        ld_wq, ld_wk, ld_wv, ld_wo = sem("ld_wq"), sem("ld_wk"), sem("ld_wv"), sem("ld_wo")
        consts = sem("consts")
        mask_ready = sem("mask_ready")
        ln_stat, ln_pow, xn_ready = sem("ln_stat"), sem("ln_pow"), sem("xn_ready")
        xnT_psum, xnT_hi_ready, xnT_ready = sem("xnT_psum"), sem("xnT_hi_ready"), sem("xnT_ready")
        xnT_whole = sem("xnT_whole")
        wq_hi_ready, wq_ready = sem("wq_hi_ready"), sem("wq_ready")
        ctxT_psum, ctxT_hi_ready, ctxT_lo_ready = sem("ctxT_psum"), sem("ctxT_hi_ready"), sem("ctxT_lo_ready")
        ctx_hi_ready, ctx_lo_ready = sem("ctx_hi_ready"), sem("ctx_lo_ready")
        wv_hi_ready, wv_ready, wo_hi_ready, wo_ready = (
            sem("wv_hi_ready"), sem("wv_ready"), sem("wo_hi_ready"), sem("wo_ready"))
        wkT_psum, wkT_hi_ready, wkT_ready = sem("wkT_psum"), sem("wkT_hi_ready"), sem("wkT_ready")
        q_psum, q_hi_ready, q_ready = sem("q_psum"), sem("q_hi_ready"), sem("q_ready")
        qk_psum, qk_hi_ready, qk_lo_ready = sem("qk_psum"), sem("qk_hi_ready"), sem("qk_lo_ready")
        scores, masked, negmax_ready, exps = sem("scores"), sem("masked"), sem("negmax_ready"), sem("exps")
        pT_psum, pT_hi_ready, pT_lo_ready = sem("pT_psum"), sem("pT_hi_ready"), sem("pT_lo_ready")
        av = sem("av")
        rden_step = sem("rden_step")
        oT_hi_ready, oT_ready, y_psum, yT_hi_ready, yT_ready, out_psum, added = (
            sem("oT_hi_ready"), sem("oT_ready"), sem("y_psum"), sem("yT_hi_ready"), sem("yT_ready"),
            sem("out_psum"), sem("added"))
        ld_wq2, ld_wkv2, ld_wd2 = sem("ld_wq2"), sem("ld_wkv2"), sem("ld_wd2")
        wq2_hi_ready, wk2_hi_ready, wd2_hi_ready = sem("wq2_hi_ready"), sem("wk2_hi_ready"), sem("wd2_hi_ready")
        wq2_ready, wk2_ready, wd2_ready = sem("wq2_ready"), sem("wk2_ready"), sem("wd2_ready")
        wv2_ready = sem("wv2_ready")
        qa_psum, qb_psum, kv2_psum = sem("qa_psum"), sem("qb_psum"), sem("kv2_psum")
        first_q, first_kv, first_qk_ready, first_qb_ready = (
            sem("first_q"), sem("first_kv"), sem("first_qk_ready"), sem("first_qb_ready"))
        qa_ready, qb_ready, k2_ready, v2_ready = sem("qa_ready"), sem("qb_ready"), sem("k2_ready"), sem("v2_ready")
        s2_psum, s2_masked, s2_negmax, s2_exps, s2_rden, s2_probs = (
            sem("s2_psum"), sem("s2_masked"), sem("s2_negmax"), sem("s2_exps"), sem("s2_rden"), sem("s2_probs"))
        p2T_psum, p2T_ready, c2_psum, c2_hi_ready, c2_ready, d2_psum, added2 = (
            sem("p2T_psum"), sem("p2T_ready"), sem("c2_psum"), sem("c2_hi_ready"), sem("c2_ready"),
            sem("d2_psum"), sem("added2"))
        ld_gate = sem("ld_gate")
        ld_gu = [sem(f"ld_gu{i}") for i in range(RING)]
        ld_dn = [sem(f"ld_dn{i}") for i in range(RING)]
        gate_split, gu_hi_ready, gu_ready = sem("gate_split"), sem("gu_hi_ready"), sem("gu_ready")
        logits, gate_exp, route_step = sem("logits"), sem("gate_exp"), sem("route_step")
        gu_psum, silu_ready, h_ready, down_psum, added3 = (
            sem("gu_psum"), sem("silu_ready"), sem("h_ready"), sem("down_psum"), sem("added3"))
        stored = sem("stored")

        block = stack.enter_context(nc.Block())

        @block.sync
        def _(sp):
            sp.dma_start(resid[:], x_v).then_inc(ld_x, 16)

            def load_q(g):
                after(sp, wq_ready, g)
                sp.dma_start(wq[:], xq_v[g]).then_inc(ld_wq, 16)
                after(sp, wkT_psum, g)
                sp.dma_start(wk[:], xk_v[g]).then_inc(ld_wk, 16)

            def load_o(g):
                after(sp, wo_ready, g)
                sp.dma_start(wv[:], xv_v[g]).then_inc(ld_wv, 16)
                sp.dma_start(wo[:], xo_v[g]).then_inc(ld_wo, 16)

            def load_mask(b):
                sp.dma_start(mask8[:, b, :], key_mask[b:b + 1, :].broadcast_to([P, KEYS])).then_inc(ld_mask[b], 16)

            def load_ctx(c):
                b, k = divmod(c, NCH)
                sp.dma_start(ctx_raw[:, c * CH:(c + 1) * CH], ctx_v[b, :, k * CH:(k + 1) * CH]).then_inc(ld_ctx[c], 16)

            load_q(0)
            load_mask(0)
            for c in range(1, B * NCH):
                load_ctx(c)
            load_mask(1)
            load_o(0)
            sp.dma_start(gatew[:], gate_w.rearrange("(k p) e -> p k e", p=P)).then_inc(ld_gate, 16)
            sp.dma_start(bias_b[:, 0, :], expert_bias.rearrange("(a e) -> a e", a=1).broadcast_to([P, E])
                         ).then_inc(ld_gate, 16)
            load_q(1)
            with sp.Fori(1, G - 1) as g:
                load_q(g + 1)
                load_o(g)
            load_o(G - 1)

            sp.wait_ge(ctxT_psum, B * NCH)
            sp.wait_ge(ctx_hi_ready, B * NCH)
            sp.wait_ge(ctx_lo_ready, B)

            def load_qkv(r):
                after(sp, wq2_ready, r)
                sp.dma_start(wq2.rearrange("p (k e) -> p k e", k=HB), sq_v[r]).then_inc(ld_wq2, 16)
                after(sp, wv2_ready, r)
                after(sp, wk2_ready, r)
                for i in range(2):
                    sp.dma_start(wkv2.rearrange("p (k s e) -> p k s e", k=HB, s=2)[:, :, i, :],
                                 skv_v[r, i]).then_inc(ld_wkv2, 16)

            def load_d(r):
                after(sp, wd2_ready, r)
                sp.dma_start(wd2.rearrange("p (h n) -> p h n", h=HR), sd_v[r]).then_inc(ld_wd2, 16)

            load_qkv(0)
            load_d(0)
            sp.dma_start(ring_gu[:, 0, :, 0:F], sh_gate_w.rearrange("(k p) f -> p k f", p=P)).then_inc(ld_gu[0], 16)
            sp.dma_start(ring_gu[:, 0, :, F:2 * F], sh_up_w.rearrange("(k p) f -> p k f", p=P)).then_inc(ld_gu[0], 16)
            sp.dma_start(ring_dn[:, 0, :], sh_down_w).then_inc(ld_dn[0], 16)
            for m in range(1, RING):
                sp.dma_start(ring_gu[:, m], exgu_v[m - 1]).then_inc(ld_gu[m], 16)
                sp.dma_start(ring_dn[:, m, :], ex_down_w[m - 1]).then_inc(ld_dn[m], 16)
            load_qkv(1)
            with sp.Fori(1, R - 1) as r:
                load_qkv(r + 1)
                load_d(r)
            load_d(R - 1)

            def load_expert(i, s):
                m = RING * i + s
                sp.wait_ge(gu_ready, m - RING + 1)
                sp.dma_start(ring_gu[:, s], exgu_v[m - 1]).then_inc(ld_gu[s], 16)
                sp.wait_ge(down_psum, m - RING + 1)
                sp.dma_start(ring_dn[:, s, :], ex_down_w[m - 1]).then_inc(ld_dn[s], 16)

            with sp.Fori(1, E // RING) as i:
                for s in range(RING):
                    load_expert(i, s)
            load_expert(E // RING, 0)

            for b in range(B):
                sp.wait_ge(added3, B * E + b + 1)
                sp.dma_start(out_v[:, b, :], resid[:, b, :]).then_inc(stored, 16)
            sp.wait_ge(stored, 16 * B)

        @block.gpsimd
        def _(pool):
            pool.memset(ident[:], 0.0).then_inc(consts, 1)
            pool.memset(causal[:], 0.0).then_inc(consts, 1)
            pool.memset(minus_half[:], -0.5).then_inc(consts, 1)
            pool.iota(rank[:, 0, :], [[-1, E]], base=E, channel_multiplier=0,
                      allow_small_or_imprecise_dtypes=True).then_inc(consts, 1)
            pool.wait_ge(consts, 4)
            pool.affine_select(out=ident[:], in_=ident[:], compare_op=ALU.not_equal, fill=1.0, base=0,
                               pattern=[[-1, P]], channel_multiplier=1).then_inc(consts, 1)
            pool.affine_select(out=causal[:], in_=causal[:], compare_op=ALU.is_ge, fill=NEG, base=0,
                               pattern=[[-1, P]], channel_multiplier=1).then_inc(consts, 1)
            pool.memset(ones[:], 1.0).then_inc(consts, 1)
            pool.wait_ge(consts, 7)

            def power(b, n):
                pool.wait_ge(ln_stat, 3 * (B * n + b + 1))
                pool.tensor_tensor(rstd[:, b], var_eps[:, b], minus_half[:], ALU.pow).then_inc(ln_pow, 1)

            def rest(dst, src, hi, ready):
                pool.tensor_tensor(dst, src, hi.bitcast(F32), ALU.subtract).then_inc(ready, 1)

            def split_wq(g):
                flat = "p k e -> p (k e)"
                after(pool, q_psum, g)
                pool.wait_ge(ld_wq, 16 * (g + 1))
                pool.tensor_tensor(wq_hi[:].rearrange(flat), wq[:].rearrange(flat), ones[:],
                                   ALU.mult).then_inc(wq_hi_ready, 1)
                pool.wait_ge(wq_hi_ready, g + 1)
                rest(wq_lo[:].rearrange(flat), wq[:].rearrange(flat), wq_hi[:].rearrange(flat), wq_ready)

            def split_o(g):
                after(pool, out_psum, 2 * g)
                pool.wait_ge(ld_wv, 16 * (g + 1))
                pool.tensor_tensor(wv_hi[:], wv[:], ones[:, 0:P], ALU.mult).then_inc(wv_hi_ready, 1)
                pool.wait_ge(ld_wo, 16 * (g + 1))
                pool.tensor_tensor(wo_hi[:], wo[:], ones[:].rearrange("p (j n) -> p j n", j=J),
                                   ALU.mult).then_inc(wo_hi_ready, 1)
                pool.wait_ge(wv_hi_ready, g + 1)
                rest(wv_lo[:], wv[:], wv_hi[:], wv_ready)
                pool.wait_ge(wo_hi_ready, g + 1)
                rest(wo_lo[:], wo[:], wo_hi[:], wo_ready)

            def ctx_rest(b):
                pool.wait_ge(ctx_hi_ready, NCH * (b + 1))
                rest(ctx_lo[:, b].rearrange("p i d -> p (i d)"), ctx_raw[:, b * KEYS:(b + 1) * KEYS],
                     ctx_hi[:, b].rearrange("p i d -> p (i d)"), ctx_lo_ready)

            def mask(b):
                pool.wait_ge(ld_mask[b], 16)
                for k in range(NCH):
                    pool.tensor_scalar(mask_bias[:, b, k * CH:(k + 1) * CH].rearrange("p (i q) -> p i q", q=P),
                                       mask8[:, b].rearrange("p (q i) -> p i q", i=NBLK)[:, 4 * k:4 * k + 4, :],
                                       -1.0, -NEG, ALU.add, ALU.mult).then_inc(mask_ready, 1)

            power(0, 0)
            power(1, 0)
            mask(0)
            ctx_rest(0)
            split_wq(1)
            mask(1)
            ctx_rest(1)
            split_o(0)
            with pool.Fori(2, G) as g:
                split_wq(g)
                split_o(g - 1)
            split_o(G - 1)

            def split_q(r):
                pool.wait_ge(wq2_hi_ready, r + 1)
                rest(wq2_lo, wq2, wq2_hi, wq2_ready)

            def split_k(r):
                pool.wait_ge(wk2_hi_ready, r + 1)
                rest(wk2_lo, wk2, wk2_hi, wk2_ready)

            def split_d(r):
                pool.wait_ge(wd2_hi_ready, r + 1)
                rest(wd2_lo, wd2, wd2_hi, wd2_ready)

            def normalise(r):
                for b in range(B):
                    pool.wait_ge(s2_rden, 2 * r + b + 1)
                    pool.tensor_tensor(p2[:, b], p2[:, b], rd2[:, b].unsqueeze(2).broadcast_to([P, HR, P]),
                                       ALU.mult).then_inc(s2_probs, 1)

            split_q(0)
            split_k(0)
            split_d(0)
            power(0, 1)
            power(1, 1)
            split_q(1)
            split_k(1)
            normalise(0)
            split_q(2)
            split_k(2)
            with pool.Fori(1, R - 2) as r:
                normalise(r)
                split_q(r + 2)
                split_k(r + 2)
                split_d(r)
            for r in range(R - 2, R):
                normalise(r)
                split_d(r)

            def split_expert(i, s):
                pool.wait_ge(gu_hi_ready, RING * i + s + 1)
                rest(gu_lo[:, s], ring_gu[:, s].rearrange("p k f -> p (k f)"), gu_hi[:, s], gu_ready)

            split_expert(0, 0)
            split_expert(0, 1)
            for b in range(B):
                power(b, 2)
            split_expert(0, 2)
            split_expert(0, 3)
            with pool.Fori(1, E // RING) as i:
                for s in range(RING):
                    split_expert(i, s)
            split_expert(E // RING, 0)

        @block.tensor
        def _(pe):
            def product(dst, w, x, start, stop):
                pe.matmul(dst, w[1], x[0], start=start, stop=False)
                pe.matmul(dst, w[0], x[1], start=False, stop=False)
                return pe.matmul(dst, w[0], x[0], start=False, stop=stop)

            def ctx_chunk(c):
                b, k = divmod(c, NCH)
                pe.wait_ge(ld_ctx[c], 16)
                if c == 0:
                    pe.wait_ge(consts, 6)
                if c >= 4:
                    pe.wait_ge(ctxT_lo_ready, c - 3)
                for i in range(4):
                    blk = b * NBLK + 4 * k + i
                    last = pe.transpose(bank[2 + c % 4][:, i * P:(i + 1) * P], ctx_raw[:, blk * P:(blk + 1) * P], ident[:])
                last.then_inc(ctxT_psum, 1)

            def xn_transpose(b, n, dst):
                pe.wait_ge(xn_ready, B * n + b + 1)
                for k in range(HB):
                    last = pe.transpose(dst[:, k * P:(k + 1) * P], xn[:, b, k * P:(k + 1) * P], ident[:])
                last.then_inc(xnT_psum, 1)

            def wk_transpose(g):
                pe.wait_ge(ld_wk, 16 * (g + 1))
                after(pe, qk_lo_ready, 2 * g)
                pe.transpose(WQK_BANK[:, 0:P], wk[:], ident[:]).then_inc(wkT_psum, 1)

            def q_project(g, j):
                if j == 0:
                    pe.wait_ge(wq_ready, g + 1)
                for k in range(HB):
                    cols = slice(j * P, (j + 1) * P)
                    last = product(QYO_BANK[:].rearrange("p (b j t) -> p j b t", b=B, j=J)[:, j],
                                   (wq_hi[:, k, cols], wq_lo[:, k, cols]),
                                   [v[:, k, :].rearrange("p (b t) -> p b t", b=B) for v in (xnT_hi, xnT_lo)],
                                   k == 0, k == HB - 1)
                if j == J - 1:
                    last.then_inc(q_psum, 1)

            def q_fold(g):
                pe.wait_ge(wkT_ready, g + 1)
                pe.wait_ge(q_ready, g + 1)
                product(WQK_BANK[:], (wkT_hi[:], wkT_lo[:]), (qT_hi[:], qT_lo[:]), True, True).then_inc(qk_psum, 1)

            def step(g, n, scores_on, trans_on, av_on, fold_on, out_on):
                N = STEPS * g + n
                if scores_on:
                    b, j, k = n // SPU, n % SPU // NCH, n % NCH
                    if n % SPU == 0:
                        pe.wait_ge(qk_hi_ready, 2 * g + b + 1)
                        pe.wait_ge(qk_lo_ready, 2 * g + b + 1)
                    after(pe, masked, N - 1)
                    keys = slice(k * CH, (k + 1) * CH)
                    pe.matmul(S_BANK[n % 2][:], qk_hi[:, b, j], ctxT_lo[:, b, keys], start=True, stop=False)
                    pe.matmul(S_BANK[n % 2][:], qk_lo[:, b, j], ctxT_hi[:, b, keys], start=False, stop=False)
                    pe.matmul(S_BANK[n % 2][:], qk_hi[:, b, j], ctxT_hi[:, b, keys],
                              start=False, stop=True).then_inc(scores, 1)
                if trans_on:
                    t = N - LAG_T
                    p, b = (n - LAG_T) % SPU, (n - LAG_T) // SPU % 2
                    if p in (0, SPU // 2):
                        pe.wait_ge(exps, 4 * (2 * g + (n - LAG_T) // SPU) + (3 if p == 0 else 4))
                    after(pe, pT_lo_ready, t - 1)
                    for i in range(2):
                        for j in range(J):
                            at = (i * J + j) * P
                            last = pe.transpose(PT_BANK[n % 2][:, at:at + P],
                                                probs[:, b, j, (2 * p + i) * P:(2 * p + i + 1) * P], ident[:])
                    last.then_inc(pT_psum, 1)
                if out_on and n in (5, 13):
                    u = 2 * (g - 1) + n // SPU
                    if n == 5:
                        pe.wait_ge(wv_ready, g)
                    pe.wait_ge(oT_ready, u + 1)
                    if not scores_on:
                        pe.wait_ge(added, 2 * u)
                    if n == 13 and fold_on:
                        pe.wait_ge(q_ready, g + 2)
                    product(QYO_BANK[:, 0:J * T], (wv_hi[:], wv_lo[:]), (oT_hi[:], oT_lo[:]),
                            True, True).then_inc(y_psum, 1)
                if out_on and n in (6, 14):
                    u = 2 * (g - 1) + n // SPU
                    if n == 6:
                        pe.wait_ge(wo_ready, g)
                    pe.wait_ge(yT_ready, u + 1)
                    for j in range(J):
                        rows = slice(j * T, (j + 1) * T)
                        last = product(QYO_BANK[:, j * H:(j + 1) * H], (yT_hi[:, rows], yT_lo[:, rows]),
                                       (wo_hi[:, j], wo_lo[:, j]), True, True)
                    last.then_inc(out_psum, 1)
                if av_on:
                    a = N - LAG_A
                    p, b = (n - LAG_A) % SPU, (n - LAG_A) // SPU % 2
                    pe.wait_ge(pT_lo_ready, a + 1)
                    s = (n - LAG_A) % PTR
                    for i in range(2):
                        blk, cols = 2 * p + i, slice(i * J * P, (i + 1) * J * P)
                        dst = O_BANK[b][:, 0:J * T]
                        pe.matmul(dst, ctx_lo[:, b, blk], pT_hi[:, s, cols], start=(blk == 0), stop=False)
                        pe.matmul(dst, ctx_hi[:, b, blk], pT_lo[:, s, cols], start=False, stop=False)
                        last = pe.matmul(dst, ctx_hi[:, b, blk], pT_hi[:, s, cols], start=False, stop=(blk == NBLK - 1))
                    last.then_inc(av, 1)
                if fold_on and n == 8:
                    wk_transpose(g + 1)
                    after(pe, added, 2 * (2 * g - 1))
                    q_project(g + 1, 0)
                if fold_on and n == 9:
                    q_project(g + 1, 1)
                if fold_on and n == 12:
                    q_fold(g + 1)

            pe.wait_ge(consts, 7)
            pe.matmul(QYO_BANK[:], ones[:, 0:P], ones[:], start=True, stop=True)
            ctx_chunk(0)
            for b in range(B):
                xn_transpose(b, 0, S_BANK[b])
            wk_transpose(0)
            ctx_chunk(1)
            pe.wait_ge(xnT_ready, B)
            q_project(0, 0)
            q_project(0, 1)
            ctx_chunk(2)
            ctx_chunk(3)
            q_fold(0)

            for n in range(STEPS):
                if n % SPU < NCH:
                    pe.wait_ge(ctxT_lo_ready, n // SPU * NCH + n % SPU + 1)
                if n == LAG_A:
                    pe.wait_ge(ctx_lo_ready, 1)
                step(0, n, True, n >= LAG_T, n >= LAG_A, True, False)
                if n < NCH:
                    ctx_chunk(NCH + n)
            pe.wait_ge(ctx_lo_ready, B)
            with pe.Fori(1, G - 1) as g:
                for n in range(STEPS):
                    step(g, n, True, True, True, True, True)
            for n in range(STEPS):
                step(G - 1, n, True, True, True, False, True)
            QA, QB, KV, D_BANK = bank[0], bank[1], bank[2], bank[7]
            SC, PC = bank[3:5], bank[5:7]
            XT = [(xnT_hi[:, k, :], xnT_lo[:, k, :]) for k in range(HB)]

            def keep_warm(where, count):
                for _ in range(count):
                    pe.matmul(where[:], pT_hi[:, 0, 0:P], pT_hi[:, 0], start=True, stop=True)

            def two_heads(dst, first, cols, done):
                for h in range(2):
                    for k in range(HB):
                        at = (k * HR + first + h) * P
                        last = product(dst[:, h * B * T + cols.start:h * B * T + cols.stop],
                                       (wq2_hi[:, at:at + P], wq2_lo[:, at:at + P]),
                                       [v[:, cols] for v in XT[k]], k == 0, k == HB - 1)
                last.then_inc(done, 1)

            def queries2(r, cols):
                pe.wait_ge(wq2_ready, r + 1)
                two_heads(QA, 0, cols, qa_psum)
                two_heads(QB, 2, cols, qb_psum)

            def keys_values2(r, cols, done):
                pe.wait_ge(wk2_ready, r + 1)
                pe.wait_ge(wv2_ready, r + 1)
                after(pe, v2_ready, r)
                for k in range(HB):
                    product(KV[:, cols], (wk2_hi[:, k], wk2_lo[:, k]), [v[:, cols] for v in XT[k]],
                            k == 0, k == HB - 1)
                if isinstance(r, int) and r == 0:
                    pe.wait_ge(xnT_whole, cols.stop // T)
                for b in range(cols.start // T, cols.stop // T):
                    for k in range(HB):
                        last = pe.matmul(KV[:, (B + b) * P:(B + b + 1) * P], xnT[:, k, b * T:(b + 1) * T],
                                         wv2[:, k], start=(k == 0), stop=(k == HB - 1))
                last.then_inc(done, 1)

            def scores2(r, b):
                for h in range(HR):
                    mm = pe.matmul(SC[b][:, h * P:(h + 1) * P], q2T[:, h, b * T:(b + 1) * T],
                                   k2T[:, b * T:(b + 1) * T], start=True, stop=True)
                mm.then_inc(s2_psum, 1)

            def attend2(r):
                pe.wait_ge(v2_ready, r + 1)
                for b in range(B):
                    pe.wait_ge(p2T_ready, 2 * r + b + 1)
                    pe.matmul(PC[b][:], v2[:, b], p2T[:, b], start=True, stop=True).then_inc(c2_psum, 1)

            def dense2(r):
                pe.wait_ge(wd2_ready, r + 1)
                for b in range(B):
                    pe.wait_ge(c2_ready, 2 * r + b + 1)
                    for h in range(HR):
                        cols = slice(h * P, (h + 1) * P)
                        mm = product(D_BANK[:, b * H:(b + 1) * H], (c2_hi[:, b, cols], c2_lo[:, b, cols]),
                                     (wd2_hi[:, h * H:(h + 1) * H], wd2_lo[:, h * H:(h + 1) * H]),
                                     h == 0, h == HR - 1)
                mm.then_inc(d2_psum, 1)

            def group2(r, before, behind):
                pe.wait_ge(qa_ready, r + 1)
                pe.wait_ge(qb_ready, r + 1)
                pe.wait_ge(k2_ready, r + 1)
                for b in range(0 if before else 1, B):
                    scores2(r, b)
                if before:
                    attend2(r - 1)
                if not behind:
                    keep_warm(QA, 8)
                if behind:
                    queries2(r + 1, both)
                if before:
                    dense2(r - 1)
                if behind:
                    keys_values2(r + 1, both, kv2_psum)
                for b in range(B):
                    pe.wait_ge(s2_probs, 2 * r + b + 1)
                    for h in range(HR):
                        mm = pe.transpose(PC[b][:, h * P:(h + 1) * P], p2[:, b, h], ident[:])
                    mm.then_inc(p2T_psum, 1)

            both, of = slice(0, B * T), [slice(b * T, (b + 1) * T) for b in range(B)]
            for n in range(STEPS):
                step(G, n, False, n < LAG_T, n < LAG_A, False, True)
                if n == LAG_T:
                    xn_transpose(0, 1, WQK_BANK)
                if n == LAG_A - 1:
                    pe.wait_ge(masked, NT)
                    pe.wait_ge(xnT_ready, B + 1)
                    pe.wait_ge(wq2_ready, 1)
                    two_heads(QA, 0, of[0], first_q)
                if n == 13:
                    two_heads(QB, 2, of[0], first_q)
                if n == 14:
                    keys_values2(0, of[0], first_kv)
                    keep_warm(bank[4], 3)
            pe.wait_ge(first_qk_ready, 2)
            pe.wait_ge(first_qb_ready, 1)
            scores2(0, 0)
            keep_warm(bank[4], 4)
            xn_transpose(1, 1, WQK_BANK)
            keep_warm(bank[4], 5)
            pe.wait_ge(xnT_ready, 2 * B)
            queries2(0, of[1])
            keys_values2(0, of[1], kv2_psum)
            group2(0, False, True)
            with pe.Fori(1, R - 1) as r:
                group2(r, True, True)
            group2(R - 1, True, False)
            keep_warm(QA, 2)
            attend2(R - 1)
            keep_warm(QA, 4)
            dense2(R - 1)
            keep_warm(QA, 16)

            GU, DWN = bank[0:2], bank[3:5]
            for b in range(B):
                xn_transpose(b, 2, (bank[2], bank[5])[b])
            keep_warm(QA, 5)
            pe.wait_ge(xnT_ready, 3 * B)

            def gate_up(i, s):
                m = RING * i + s
                pe.wait_ge(gu_ready, m + 1)
                after(pe, h_ready, m - 1)
                for half in range(2):
                    for k in range(HB):
                        at = (2 * k + half) * F
                        mm = product(GU[s % 2][:, half * B * T:(half + 1) * B * T],
                                     (gu_hi[:, s, at:at + F], gu_lo[:, s, at:at + F]), XT[k], k == 0, k == HB - 1)
                mm.then_inc(gu_psum, 1)

            def down(i, s):
                m = RING * i + s
                pe.wait_ge(ld_dn[s], 16 * (i + 1))
                pe.wait_ge(h_ready, m + 1)
                after(pe, added3, B * (m - 1))
                for b in range(B):
                    mm = pe.matmul(DWN[s % 2][:, b * H:(b + 1) * H], hT[:, s % 2, b * T:(b + 1) * T],
                                   ring_dn[:, s, :], start=True, stop=True)
                mm.then_inc(down_psum, 1)

            pe.wait_ge(gate_split, 2)
            for b in range(B):
                rows = slice(b * T, (b + 1) * T)
                for k in range(HB):
                    for n, (xv, wv_) in enumerate(((xnT_lo, gatew_lo), (xnT_lo, gatew_hi),
                                                   (xnT_hi, gatew_lo), (xnT_hi, gatew_hi))):
                        mm = pe.matmul(bank[6][:, b * E:(b + 1) * E], xv[:, k, rows], wv_[:, k, :],
                                       start=(k == 0 and n == 0), stop=(k == HB - 1 and n == 3))
            mm.then_inc(logits, 1)
            gate_up(0, 0)
            for s in range(1, RING):
                gate_up(0, s)
                down(0, s - 1)
            with pe.Fori(1, E // RING) as i:
                for s in range(RING):
                    gate_up(i, s)
                    if s == 0:
                        down(i - 1, RING - 1)
                    else:
                        down(i, s - 1)
            gate_up(E // RING, 0)
            down(E // RING - 1, RING - 1)
            down(E // RING, 0)

        @block.scalar
        def _(act):
            act.preload_act_table(ACT.Exp)
            act.dma_start(ctx_raw[:, 0:CH], ctx_v[0, :, 0:CH]).then_inc(ld_ctx[0], 16)

            def ctx_chunk(c):
                b, k = divmod(c, NCH)
                act.wait_ge(ctxT_psum, c + 1)
                act.activation(ctxT_hi[:, b, k * CH:(k + 1) * CH], bank[2 + c % 4][:], ACT.Copy).then_inc(ctxT_hi_ready, 1)

            def ctx_round(c):
                b, k = divmod(c, NCH)
                act.wait_ge(ld_ctx[c], 16)
                act.activation(ctx_hi[:, b, 4 * k:4 * k + 4].rearrange("p i d -> p (i d)"),
                               ctx_raw[:, c * CH:(c + 1) * CH], ACT.Copy).then_inc(ctx_hi_ready, 1)

            def xnT_copy(b, n, src):
                act.wait_ge(xnT_psum, B * n + b + 1)
                rows = src[:, 0:HB * P].rearrange("p (k t) -> p k t", k=HB)
                act.activation(xnT_hi[:, :, b * T:(b + 1) * T], rows, ACT.Copy).then_inc(xnT_hi_ready, 1)
                return rows

            def xnT_copy_whole(b, rows):
                act.wait_ge(xnT_ready, B + b + 1)
                act.activation(xnT[:, :, b * T:(b + 1) * T], rows, ACT.Copy).then_inc(xnT_whole, 1)

            def wkT_copy(g):
                act.wait_ge(wkT_psum, g + 1)
                act.activation(wkT_hi[:], WQK_BANK[:, 0:P], ACT.Copy).then_inc(wkT_hi_ready, 1)

            def q_copy(g):
                act.wait_ge(q_psum, g + 1)
                act.activation(qT_hi[:], QYO_BANK[:], ACT.Copy).then_inc(q_hi_ready, 1)

            def fold_copy(g, b):
                if b == 0:
                    act.wait_ge(qk_psum, g + 1)
                else:
                    act.wait_ge(qk_lo_ready, 2 * g + 1)
                after(act, scores, STEPS * (g - 1) + SPU * (b + 1))
                act.activation(qk_hi[:, b].rearrange("p j t -> p (j t)"), WQK_BANK[:, b * J * T:(b + 1) * J * T],
                               ACT.Copy).then_inc(qk_hi_ready, 1)

            def exp_half(g, du, j, half):
                u = 2 * g + du
                b = du % 2
                if half == 0:
                    act.wait_ge(negmax_ready, 2 * u + j + 1)
                part = probs[:, b, j, half * (KEYS // 2):(half + 1) * (KEYS // 2)]
                act.activation(part, part, ACT.Exp, bias=negmax[:, b, j:j + 1], scale=SCALE,
                               accum_out=den[:, b, j, half:half + 1]).then_inc(exps, 1)

            EXPS = {1: (-1, 1, 0), 3: (-1, 1, 1), 5: (0, 0, 0), 7: (0, 0, 1),
                    9: (0, 1, 0), 11: (0, 1, 1), 13: (1, 0, 0), 15: (1, 0, 1)}

            def step(g, n, exp_on, trans_on, fold_on, fold2_on, out_on):
                t = STEPS * g + n - LAG_T
                if out_on and n in (4, 12):
                    u = 2 * (g - 1) + n // SPU
                    act.wait_ge(av, SPU * (u + 1))
                    act.activation(oT_hi[:], O_BANK[n // SPU][:, 0:J * T], ACT.Copy).then_inc(oT_hi_ready, 1)
                if out_on and n in (5, 13):
                    u = 2 * (g - 1) + n // SPU
                    act.wait_ge(y_psum, u + 1)
                    act.activation(yT_hi[:], QYO_BANK[:, 0:J * T], ACT.Copy).then_inc(yT_hi_ready, 1)
                if exp_on and n in EXPS:
                    exp_half(g, *EXPS[n])
                if trans_on:
                    after(act, av, t - PTR + 1)
                    act.wait_ge(pT_psum, t + 1)
                    act.activation(pT_hi[:, (n - LAG_T) % PTR], PT_BANK[n % 2][:], ACT.Copy).then_inc(pT_hi_ready, 1)
                if fold2_on and n == 0:
                    fold_copy(g, 1)
                if fold_on and n == 9:
                    wkT_copy(g + 1)
                if fold_on and n == 10:
                    q_copy(g + 1)
                if fold_on and n == 13:
                    fold_copy(g + 1, 0)

            act.wait_ge(ld_wq, 16)
            act.activation(wq_hi[:], wq[:], ACT.Copy).then_inc(wq_hi_ready, 1)
            ctx_chunk(0)
            for b in range(B):
                xnT_copy(b, 0, S_BANK[b])
            wkT_copy(0)
            ctx_chunk(1)
            ctx_round(0)
            q_copy(0)
            ctx_chunk(2)
            ctx_chunk(3)
            fold_copy(0, 0)
            for c in range(1, NCH):
                ctx_round(c)

            for n in range(STEPS):
                if n < NCH:
                    step(0, n, False, False, True, True, False)
                    ctx_chunk(NCH + n)
                    ctx_round(NCH + n)
                else:
                    step(0, n, n >= 5, n >= LAG_T, True, True, False)
            with act.Fori(1, G - 1) as g:
                for n in range(STEPS):
                    step(g, n, True, True, True, True, True)
            for n in range(STEPS):
                step(G - 1, n, True, True, False, True, True)
            QA, KV, PC = bank[0], bank[2], bank[5:7]

            def q_half(cols):
                return QA[:].rearrange("p (h t) -> p h t", h=2)[:, :, cols]

            def copy_qk(r):
                after(act, s2_psum, 2 * r)
                act.wait_ge(qa_psum, r + 1)
                act.activation(q2T[:, 0:2].rearrange("p h t -> p (h t)"), QA[:], ACT.Copy).then_inc(qa_ready, 1)
                act.wait_ge(kv2_psum, r + 1)
                act.activation(k2T, KV[:, 0:B * T], ACT.Copy).then_inc(k2_ready, 1)

            def exps2(r, b):
                act.wait_ge(s2_negmax, 2 * r + b + 1)
                for h in range(HR):
                    act.activation(p2[:, b, h], p2[:, b, h], ACT.Exp, bias=nm2[:, b, h:h + 1],
                                   accum_out=ds2[:, b, h:h + 1]).then_inc(s2_exps, 1)

            def copy_c(r):
                for b in range(B):
                    act.wait_ge(c2_psum, 2 * r + b + 1)
                    act.activation(c2_hi[:, b], PC[b][:], ACT.Copy).then_inc(c2_hi_ready, 1)

            def group2(r, before, behind):
                if before:
                    exps2(r, 0)
                if before:
                    copy_c(r - 1)
                exps2(r, 1)
                if behind:
                    copy_qk(r + 1)
                for b in range(B):
                    act.wait_ge(p2T_psum, 2 * r + b + 1)
                    act.activation(p2T[:, b], PC[b][:], ACT.Copy).then_inc(p2T_ready, 1)

            for n in range(STEPS):
                step(G, n, n < 5, n < LAG_T, False, False, True)
                if n == LAG_T:
                    xnT_copy_whole(0, xnT_copy(0, 1, WQK_BANK))
                if n == LAG_A:
                    act.wait_ge(first_q, 1)
                    act.activation(q2T[:, 0:2, 0:T], q_half(slice(0, T)), ACT.Copy).then_inc(first_qk_ready, 1)
            act.wait_ge(first_kv, 1)
            act.activation(k2T[:, 0:T], KV[:, 0:T], ACT.Copy).then_inc(first_qk_ready, 1)
            xnT_rows = xnT_copy(1, 1, WQK_BANK)
            exps2(0, 0)
            xnT_copy_whole(1, xnT_rows)
            act.wait_ge(qa_psum, 1)
            act.activation(q2T[:, 0:2, T:2 * T], q_half(slice(T, 2 * T)), ACT.Copy).then_inc(qa_ready, 1)
            act.wait_ge(kv2_psum, 1)
            act.activation(k2T[:, T:2 * T], KV[:, T:2 * T], ACT.Copy).then_inc(k2_ready, 1)
            group2(0, False, True)
            with act.Fori(1, R - 1) as r:
                group2(r, True, True)
            group2(R - 1, True, False)
            copy_c(R - 1)

            GU = bank[0:2]
            def silu(m, s):
                after(act, h_ready, m - 1)
                act.wait_ge(gu_psum, m + 1)
                act.activation(sg[:, s % 2], GU[s % 2][:, 0:B * T], ACT.Silu).then_inc(silu_ready, 1)

            for b in range(B):
                xnT_copy(b, 2, (bank[2], bank[5])[b])
            act.wait_ge(logits, 1)
            act.activation(sc.rearrange("p b e -> p (b e)"), bank[6][:, 0:B * E], ACT.Exp,
                           scale=-1.0).then_inc(gate_exp, 1)

            for s in range(RING):
                silu(s, s)
            with act.Fori(1, E // RING) as i:
                for s in range(RING):
                    silu(RING * i + s, s)
            silu(E, 0)

        @block.vector
        def _(dve):
            def norm_stats(b, n):
                o = 3 * (B * n + b)
                dve.bn_stats(stats[:, b, :], resid[:, b, :]).then_inc(ln_stat, 1)
                dve.wait_ge(ln_stat, o + 1)
                dve.bn_aggr(meanvar[:, b, :], stats[:, b, :]).then_inc(ln_stat, 1)
                dve.wait_ge(ln_stat, o + 2)
                dve.tensor_scalar(var_eps[:, b], meanvar[:, b, 1:2], EPS, None, ALU.add).then_inc(ln_stat, 1)

            def norm_apply(b, n):
                dve.wait_ge(ln_pow, B * n + b + 1)
                after(dve, xnT_psum, B * (n - 1) + b + 1)
                dve.tensor_scalar(xn[:, b, :], resid[:, b, :], meanvar[:, b, 0:1], rstd[:, b],
                                  ALU.subtract, ALU.mult).then_inc(xn_ready, 1)

            def xnT_rest(b, n, src):
                dve.wait_ge(xnT_hi_ready, B * n + b + 1)
                dve.tensor_tensor(xnT_lo[:, :, b * T:(b + 1) * T], src[:, 0:HB * P].rearrange("p (k t) -> p k t", k=HB),
                                  xnT_hi[:, :, b * T:(b + 1) * T].bitcast(F32), ALU.subtract).then_inc(xnT_ready, 1)

            def ctx_chunk(c):
                b, k = divmod(c, NCH)
                dve.wait_ge(ctxT_hi_ready, c + 1)
                cols = slice(k * CH, (k + 1) * CH)
                dve.tensor_tensor(ctxT_lo[:, b, cols], bank[2 + c % 4][:], ctxT_hi[:, b, cols].bitcast(F32),
                                  ALU.subtract).then_inc(ctxT_lo_ready, 1)

            def fold_rest(g, b):
                dve.wait_ge(qk_hi_ready, 2 * g + b + 1)
                dve.tensor_tensor(qk_lo[:, b].rearrange("p j t -> p (j t)"), WQK_BANK[:, b * J * T:(b + 1) * J * T],
                                  qk_hi[:, b].bitcast(F32).rearrange("p j t -> p (j t)"),
                                  ALU.subtract).then_inc(qk_lo_ready, 1)

            def rest_of(lo, src, hi, hi_ready, count, ready):
                dve.wait_ge(hi_ready, count + 1)
                dve.tensor_tensor(lo[:], src[:, 0:lo.shape[1]], hi[:].bitcast(F32), ALU.subtract).then_inc(ready, 1)

            def wkT_rest(g):
                rest_of(wkT_lo, WQK_BANK, wkT_hi, wkT_hi_ready, g, wkT_ready)

            def q_rest(g):
                rest_of(qT_lo, QYO_BANK, qT_hi, q_hi_ready, g, q_ready)

            def denominators(g, du):
                u, b = 2 * g + du, du % 2
                dve.wait_ge(exps, 4 * u + 4)
                dve.tensor_tensor(dsum[:, b], den[:, b, :, 0], den[:, b, :, 1], ALU.add).then_inc(rden_step, 1)
                dve.wait_ge(rden_step, 3 * u + 1)
                dve.reciprocal(dsum[:, b], dsum[:, b]).then_inc(rden_step, 1)
                dve.wait_ge(rden_step, 3 * u + 2)
                dve.scalar_tensor_tensor(rden[:, b], rmax[:, b, :, NCH - 1], NEG / 2, dsum[:, b],
                                         ALU.is_gt, ALU.mult).then_inc(rden_step, 1)

            EDGE = 9

            def step(g, n, scores_on, trans_on, fold_on, fold2_on, rden_on, out_on):
                N = STEPS * g + n
                t = N - 1 - LAG_T
                if scores_on:
                    b, j, k = n // SPU, n % SPU // NCH, n % NCH
                    dve.wait_ge(scores, N + 1)
                    after(dve, masked, N)
                if trans_on:
                    dve.wait_ge(pT_hi_ready, t + 1)
                    dve.tensor_tensor(pT_lo[:, (n - 1 - LAG_T) % PTR], PT_BANK[(n - 1) % 2][:],
                                      pT_hi[:, (n - 1 - LAG_T) % PTR].bitcast(F32),
                                      ALU.subtract).then_inc(pT_lo_ready, 1)
                if scores_on:
                    keys = slice(k * CH, (k + 1) * CH)
                    dve.tensor_tensor_reduce(out=probs[:, b, j, keys], in0=S_BANK[n % 2][:], in1=mask_bias[:, b, keys],
                                             scale=1.0, scalar=(NEG if k == 0 else rmax[:, b, j, k - 1:k]),
                                             op0=ALU.add, op1=ALU.max,
                                             accum_out=rmax[:, b, j, k:k + 1]).then_inc(masked, 1)
                    if k == NCH - 1:
                        dve.wait_ge(masked, N + 1)
                        dve.tensor_scalar(negmax[:, b, j:j + 1], rmax[:, b, j, k:k + 1], -SCALE, None,
                                          ALU.mult).then_inc(negmax_ready, 1)
                if fold2_on and n == 1:
                    fold_rest(g, 1)
                if fold_on and n == 14:
                    fold_rest(g + 1, 0)
                if fold_on and n == 9:
                    wkT_rest(g + 1)
                if fold_on and n == 11:
                    q_rest(g + 1)
                if out_on and n in (4, 12):
                    u = 2 * (g - 1) + n // SPU
                    rest_of(oT_lo, O_BANK[n // SPU], oT_hi, oT_hi_ready, u, oT_ready)
                if out_on and n in (5, 13):
                    u = 2 * (g - 1) + n // SPU
                    rest_of(yT_lo, QYO_BANK, yT_hi, yT_hi_ready, u, yT_ready)
                if rden_on and n == 5:
                    denominators(g, -1)
                if rden_on and n == 13:
                    denominators(g, 0)
                if out_on and n in (6, 14):
                    b = n // SPU
                    u = 2 * (g - 1) + b
                    dve.wait_ge(out_psum, u + 1)
                    for j in range(J):
                        if j:
                            dve.wait_ge(added, 2 * u + 1)
                        dve.scalar_tensor_tensor(resid[:, b, :], QYO_BANK[:, j * H:(j + 1) * H], rden[:, b, j:j + 1],
                                                 resid[:, b, :], ALU.mult, ALU.add).then_inc(added, 1)

            QB, KV, D_BANK = bank[1], bank[2], bank[7]
            SC, PC = bank[3:5], bank[5:7]

            def first_qb(b, done, count, ready):
                cols = slice(b * T, (b + 1) * T)
                dve.wait_ge(done, count)
                dve.tensor_copy(q2T[:, 2:4, cols],
                                QB[:].rearrange("p (h t) -> p h t", h=2)[:, :, cols]).then_inc(ready, 1)

            def scale2(r, b):
                dve.wait_ge(s2_psum, 2 * r + b + 1)
                dve.scalar_tensor_tensor(p2[:, b], SC[b][:].rearrange("p (h k) -> p h k", h=HR), SCALE,
                                         causal[:].unsqueeze(1).broadcast_to([P, HR, P]),
                                         ALU.mult, ALU.add).then_inc(s2_masked, 1)

            def max2(r, b):
                dve.wait_ge(s2_masked, 2 * r + b + 1)
                dve.tensor_reduce(nm2[:, b], p2[:, b], AX.X, ALU.max, negate=True).then_inc(s2_negmax, 1)

            def round_to(hi, raw, ready):
                dve.tensor_copy(hi, raw).then_inc(ready, 1)

            def round_q(r):
                after(dve, qb_psum, r)
                dve.wait_ge(ld_wq2, 16 * (r + 1))
                round_to(wq2_hi, wq2, wq2_hi_ready)

            def round_kv(r):
                after(dve, kv2_psum, r)
                dve.wait_ge(ld_wkv2, 32 * (r + 1))
                round_to(wk2_hi, wk2, wk2_hi_ready)
                dve.tensor_copy(wv2, wv2_raw).then_inc(wv2_ready, 1)

            def round_d(r):
                after(dve, d2_psum, r)
                dve.wait_ge(ld_wd2, 16 * (r + 1))
                round_to(wd2_hi, wd2, wd2_hi_ready)

            dve.wait_ge(ld_x, 16)
            norm_stats(0, 0)
            norm_stats(1, 0)
            norm_apply(0, 0)
            norm_apply(1, 0)
            dve.wait_ge(wq_hi_ready, 1)
            dve.tensor_tensor(wq_lo[:], wq[:], wq_hi[:].bitcast(F32), ALU.subtract).then_inc(wq_ready, 1)
            for b in range(B):
                xnT_rest(b, 0, S_BANK[b])
            ctx_chunk(0)
            wkT_rest(0)
            ctx_chunk(1)
            q_rest(0)
            ctx_chunk(2)
            ctx_chunk(3)
            fold_rest(0, 0)

            for n in range(STEPS):
                if n % SPU < NCH:
                    dve.wait_ge(mask_ready, n // SPU * NCH + n % SPU + 1)
                step(0, n, True, n > LAG_T, True, True, n == 13, False)
                if n < NCH:
                    ctx_chunk(NCH + n)
            for n in range(EDGE):
                step(1, n, True, True, True, True, True, True)
            with dve.Fori(1, G - 1) as g:
                for n in range(EDGE, STEPS):
                    step(g, n, True, True, True, True, True, True)
                for n in range(EDGE):
                    step(g + 1, n, True, True, True, True, True, True)
            for n in range(EDGE, STEPS):
                step(G - 1, n, True, True, False, True, True, True)
            for n in range(STEPS):
                step(G, n, False, n <= LAG_T, False, False, n == 5, True)
                if n == 0:
                    dve.wait_ge(scores, NT)
                    round_q(0)
                if n == 2:
                    round_kv(0)
                if n == 3:
                    round_d(0)
                if n in (7, 15):
                    b = n // SPU
                    dve.wait_ge(added, 2 * (2 * (G - 1) + b + 1))
                    norm_stats(b, 1)
                if n == 8:
                    norm_apply(0, 1)
                if n == LAG_T:
                    xnT_rest(0, 1, WQK_BANK)
                if n == 14:
                    first_qb(0, first_q, 2, first_qb_ready)
            scale2(0, 0)
            norm_apply(1, 1)
            max2(0, 0)
            xnT_rest(1, 1, WQK_BANK)
            first_qb(1, qb_psum, 1, qb_ready)

            def copy_qb(r):
                after(dve, s2_psum, 2 * r)
                dve.wait_ge(qb_psum, r + 1)
                dve.tensor_copy(q2T[:, 2:4].rearrange("p h t -> p (h t)"), QB[:]).then_inc(qb_ready, 1)

            def copy_v(r):
                after(dve, c2_psum, 2 * r)
                dve.wait_ge(k2_ready, r + 1)
                dve.tensor_copy(v2.rearrange("p b d -> p (b d)"), KV[:, B * P:2 * B * P]).then_inc(v2_ready, 1)

            def rest_c(r):
                for b in range(B):
                    dve.wait_ge(c2_hi_ready, 2 * r + b + 1)
                    dve.tensor_tensor(c2_lo[:, b], PC[b][:], c2_hi[:, b].bitcast(F32),
                                      ALU.subtract).then_inc(c2_ready, 1)

            def add2(r):
                dve.wait_ge(d2_psum, r + 1)
                rows = resid[:].rearrange("p b n -> p (b n)")
                dve.tensor_tensor(rows, D_BANK[:], rows, ALU.add).then_inc(added2, 1)

            def group2(r, before, behind, split):
                for b in range(0 if before else 1, B):
                    scale2(r, b)
                    max2(r, b)
                copy_v(r)
                if before:
                    rest_c(r - 1)
                for b in range(B):
                    dve.wait_ge(s2_exps, HR * (2 * r + b + 1))
                    dve.reciprocal(rd2[:, b], ds2[:, b]).then_inc(s2_rden, 1)
                if split:
                    round_q(r + 2)
                if before:
                    add2(r - 1)
                if behind:
                    copy_qb(r + 1)
                if split:
                    round_kv(r + 2)
                if before:
                    round_d(r)

            round_q(1)
            round_kv(1)
            group2(0, False, True, True)
            with dve.Fori(1, R - 2) as r:
                group2(r, True, True, True)
            group2(R - 2, True, True, False)
            group2(R - 1, True, False, False)
            rest_c(R - 1)

            GU, DWN = bank[0:2], bank[3:5]

            def round_expert(m, s, fill):
                after(dve, gu_psum, m - RING + 1)
                dve.wait_ge(ld_gu[s], fill)
                dve.tensor_copy(gu_hi[:, s], ring_gu[:, s].rearrange("p k f -> p (k f)")).then_inc(gu_hi_ready, 1)

            for s in range(RING):
                round_expert(s, s, 32 if s == 0 else 16)
            dve.wait_ge(ld_gate, 32)
            dve.tensor_copy(gatew_hi[:], gatew[:]).then_inc(gate_split, 1)
            dve.wait_ge(gate_split, 1)
            dve.tensor_tensor(gatew_lo[:], gatew[:], gatew_hi[:].bitcast(F32), ALU.subtract).then_inc(gate_split, 1)
            add2(R - 1)
            dve.wait_ge(added2, R)
            for b in range(B):
                norm_stats(b, 2)
            for b in range(B):
                norm_apply(b, 2)
            for b in range(B):
                xnT_rest(b, 2, (bank[2], bank[5])[b])

            biased, eq, cand, hot1, hot2, comb = (route[:, i] for i in range(1, 7))
            top1, at1, top2, at2, total, rtotal = (r1[:, i] for i in range(6))

            def wide(v):
                return v.broadcast_to([P, B, E])

            flow = [0]

            def chained(ins):
                flow[0] += 1
                ins.then_inc(route_step, 1)
                dve.wait_ge(route_step, flow[0])

            def gated(m, s):
                after(dve, down_psum, m - 1)
                dve.wait_ge(silu_ready, m + 1)
                dve.tensor_tensor(hT[:, s % 2], GU[s % 2][:, B * T:2 * B * T], sg[:, s % 2],
                                  ALU.mult).then_inc(h_ready, 1)

            def router():
                dve.wait_ge(gate_exp, 1)
                chained(dve.tensor_scalar(sc, sc, 1.0, None, ALU.add))
                chained(dve.reciprocal(sc, sc))
                chained(dve.tensor_tensor(biased, sc, bias_b[:].broadcast_to([P, B, E]), ALU.add))
                for top, at, hot in ((top1, at1, hot1), (top2, at2, hot2)):
                    chained(dve.tensor_reduce(top, biased, AX.X, ALU.max))
                    chained(dve.tensor_tensor(eq, biased, wide(top), ALU.is_equal))
                    chained(dve.tensor_tensor(cand, eq, rank[:].broadcast_to([P, B, E]), ALU.mult))
                    chained(dve.tensor_reduce(at, cand, AX.X, ALU.max))
                    chained(dve.tensor_tensor(hot, cand, wide(at), ALU.is_equal))
                    gated(*((0, 0) if hot is hot1 else (1, 1)))
                    if hot is hot1:
                        chained(dve.scalar_tensor_tensor(biased, hot1, NEG, biased, ALU.mult, ALU.add))
                chained(dve.tensor_tensor(hot1, hot1, hot2, ALU.add))
                chained(dve.tensor_tensor(comb, hot1, sc, ALU.mult))
                chained(dve.tensor_reduce(total, comb, AX.X, ALU.add))
                chained(dve.tensor_scalar(total, total, 1e-20, None, ALU.add))
                chained(dve.reciprocal(rtotal, total))
                chained(dve.tensor_tensor(comb, comb, wide(rtotal), ALU.mult))

            def add_expert(m, s):
                dve.wait_ge(down_psum, m + 1)
                for b in range(B):
                    dve.wait_ge(added3, B * (m - 1) + b + 1)
                    dve.scalar_tensor_tensor(resid[:, b, :], DWN[s % 2][:, b * H:(b + 1) * H],
                                             comb[:, b, bass.ds(m - 1, 1)], resid[:, b, :],
                                             ALU.mult, ALU.add).then_inc(added3, 1)

            def unit(i, s, rounds):
                m = RING * i + s
                gated(m, s)
                add_expert(m - 1, (s - 1) % RING)
                if rounds:
                    t = (s + 3) % RING
                    ahead = i + (s + 3) // RING
                    round_expert(m + 3, t, 16 * ahead + (32 if t == 0 else 16))

            router()
            dve.wait_ge(down_psum, 1)
            for b in range(B):
                dve.tensor_tensor(resid[:, b, :], DWN[0][:, b * H:(b + 1) * H], resid[:, b, :],
                                  ALU.add).then_inc(added3, 1)
            round_expert(4, 0, 48)
            for s in range(2, RING):
                unit(0, s, True)
            with dve.Fori(1, E // RING - 1) as i:
                for s in range(RING):
                    unit(i, s, True)
            for s in range(RING):
                unit(E // RING - 1, s, s < 2)
            gated(E, 0)
            add_expert(E - 1, RING - 1)
            add_expert(E, 0)


_INS = ['x', 'ctx_1024', 'mask_BxS2_bf1', 'L0_xattn_Wq', 'L0_xattn_Wk', 'L0_xattn_Wv', 'L0_xattn_Wo',
        'L0_attn_w_q', 'L0_attn_w_kv', 'L0_attn_w_dense', 'L0_ffn_gate_w', 'L0_ffn_expert_bias',
        'L0_ffn_shared_gate_w', 'L0_ffn_shared_up_w', 'L0_ffn_shared_down_w', 'L0_ffn_experts_gate_up',
        'L0_ffn_experts_down']
_OUTS = [((2, 128, 256), 'float32')]


def kernel(**inputs):
    import numpy as _np
    import concourse.bacc as _bacc
    from concourse import mybir as _mybir
    from concourse.bass_utils import run_bass_kernel_spmd as _run

    nc = _bacc.Bacc("TRN2", target_bir_lowering=False, num_devices=1)
    arrays, args = {}, []
    for name in _INS:
        a = _np.ascontiguousarray(inputs[name])
        arrays[f"in_{name}_dram"] = a
        args.append(nc.dram_tensor(f"in_{name}_dram", a.shape, _mybir.dt.from_np(a.dtype), kind="ExternalInput").ap())
    for i, (shape, dtype) in enumerate(_OUTS):
        dt = _mybir.dt.from_np(_np.dtype(dtype))
        args.append(nc.dram_tensor(f"out_{i}_dram", shape, dt, kind="ExternalOutput").ap())
    perceiver_layer(nc, *args)
    r = _run(nc, [arrays], core_ids=[0])
    got = tuple(r.results[0][f"out_{i}_dram"] for i in range(len(_OUTS)))
    return got[0]
```

```python
from contextlib import ExitStack

import concourse.bass as bass
from concourse import mybir

ALU = mybir.AluOpType
ACT = mybir.ActivationFunctionType
AX = mybir.AxisListType
F32 = mybir.dt.float32
F32R = mybir.dt.float32r
U8 = mybir.dt.uint8

P = 128
NEG = -1e38
EPS = 1e-5


def after(eng, sem, value):
    if not isinstance(value, int) or value > 0:
        eng.wait_ge(sem, value)


def perceiver_layer(nc, x, ctx_tokens, key_mask, xq_w, xk_w, xv_w, xo_w, sq_w, skv_w, sd_w,
                    gate_w, expert_bias, sh_gate_w, sh_up_w, sh_down_w, ex_gu_w, ex_down_w, out):
    B, T, H = x.shape
    _, KEYS, VIS = ctx_tokens.shape
    assert B == 2 and T == P and VIS == P and H == 2 * P
    HB = H // P
    XH = xq_w.shape[1] // P
    G = xk_w.shape[1] // P
    J = XH // G
    NBLK = KEYS // P
    CH = 512
    NCH = KEYS // CH
    SCALE = float(P) ** -0.5
    SH = sq_w.shape[1] // P
    R = skv_w.shape[1] // (2 * P)
    HR = SH // R
    E = gate_w.shape[1]
    F = ex_down_w.shape[1]
    RING = 4
    assert J == 2 and NCH == 4 and HR == 4 and F == P and E % RING == 0

    SPU = J * NCH
    STEPS = 2 * SPU
    LAG_T = SPU + 2
    LAG_A = LAG_T + 2
    NT = G * STEPS
    PTR = 4

    xq_v = xq_w.rearrange("(k p) (g e) -> g p k e", p=P, g=G)
    xk_v = xk_w.rearrange("p (g e) -> g p e", g=G)
    xv_v = xv_w.rearrange("p (g e) -> g p e", g=G)
    xo_v = xo_w.rearrange("(g j p) n -> g p j n", p=P, g=G)
    sq_v = sq_w.rearrange("(k p) (r e) -> r p k e", p=P, r=R)
    skv_v = skv_w.rearrange("(k p) (s r e) -> r s p k e", p=P, s=2, r=R)
    sd_v = sd_w.rearrange("(r h p) n -> r p h n", p=P, r=R)
    exgu_v = ex_gu_w.rearrange("e (k p) f -> e p k f", p=P)
    x_v = x.rearrange("b t d -> t b d")
    out_v = out.rearrange("b t d -> t b d")
    ctx_v = ctx_tokens.rearrange("b (p i) d -> b p (i d)", p=P)

    with ExitStack() as stack:
        def sb(name, shape, dt=F32):
            return stack.enter_context(nc.sbuf_tensor(name, shape, dt))

        def sem(name):
            return stack.enter_context(nc.semaphore(name))

        resid = sb("resid", [P, B, H])
        xn = sb("xn", [P, B, H])
        xnT_hi = sb("xnT_hi", [P, HB, B * T], F32R)
        xnT_lo = sb("xnT_lo", [P, HB, B * T], F32R)
        xnT = sb("xnT", [P, HB, B * T])
        ones = sb("ones", [P, CH])
        ident = sb("ident", [P, P])
        causal = sb("causal", [P, P])
        minus_half = sb("minus_half", [P, 1])
        ctx_raw = sb("ctx_raw", [P, B * KEYS])
        ctx_hi = sb("ctx_hi", [P, B, NBLK, P], F32R)
        ctx_lo = sb("ctx_lo", [P, B, NBLK, P], F32R)
        ctxT_hi = sb("ctxT_hi", [P, B, KEYS], F32R)
        ctxT_lo = sb("ctxT_lo", [P, B, KEYS], F32R)
        mask8 = sb("mask8", [P, B, KEYS], U8)
        mask_bias = sb("mask_bias", [P, B, KEYS])
        probs = sb("probs", [P, B, J, KEYS])
        pT_hi = sb("pT_hi", [P, PTR, CH], F32R)
        pT_lo = sb("pT_lo", [P, PTR, CH], F32R)
        wq = sb("wq", [P, HB, J * P])
        wq_hi = sb("wq_hi", [P, HB, J * P], F32R)
        wq_lo = sb("wq_lo", [P, HB, J * P], F32R)
        wk = sb("wk", [P, P])
        wv = sb("wv", [P, P])
        wo = sb("wo", [P, J, H])
        wv_hi, wv_lo = sb("wv_hi", [P, P], F32R), sb("wv_lo", [P, P], F32R)
        wo_hi, wo_lo = sb("wo_hi", [P, J, H], F32R), sb("wo_lo", [P, J, H], F32R)
        wkT_hi, wkT_lo = sb("wkT_hi", [P, P], F32R), sb("wkT_lo", [P, P], F32R)
        qT_hi, qT_lo = sb("qT_hi", [P, B * J * T], F32R), sb("qT_lo", [P, B * J * T], F32R)
        qk_hi = sb("qk_hi", [P, B, J, T], F32R)
        qk_lo = sb("qk_lo", [P, B, J, T], F32R)
        oT_hi, oT_lo = sb("oT_hi", [P, J * T], F32R), sb("oT_lo", [P, J * T], F32R)
        yT_hi, yT_lo = sb("yT_hi", [P, J * T], F32R), sb("yT_lo", [P, J * T], F32R)
        stats = sb("stats", [P, B, 6])
        meanvar = sb("meanvar", [P, B, 2])
        var_eps = sb("var_eps", [P, B, 1])
        rstd = sb("rstd", [P, B, 1])
        rmax = sb("rmax", [P, B, J, NCH])
        negmax = sb("negmax", [P, B, J])
        den = sb("den", [P, B, J, 2])
        dsum = sb("dsum", [P, B, J])
        rden = sb("rden", [P, B, J])
        ring_gu = sb("ring_gu", [P, RING, HB, 2 * F])
        ring_dn = sb("ring_dn", [P, RING, H])
        gatew = sb("gatew", [P, HB, E])
        bias_b = sb("bias_b", [P, 1, E])
        rank = sb("rank", [P, 1, E])
        route = sb("route", [P, 7, B, E])
        r1 = sb("r1", [P, 6, B, 1])
        sc = route[:, 0]

        wq2 = ctx_raw[:, 0:1024]
        wkv2 = ctx_raw[:, 1024:1536]
        wd2 = ctx_raw[:, 1536:2560]
        parts_hi = ctxT_hi[:].rearrange("p b k -> p (b k)")
        parts_lo = ctxT_lo[:].rearrange("p b k -> p (b k)")
        wq2_hi, wq2_lo = parts_hi[:, 0:1024], parts_lo[:, 0:1024]
        wk2_hi, wk2_lo = (v[:, 1024:1280].rearrange("p (k e) -> p k e", k=HB) for v in (parts_hi, parts_lo))
        wk2 = wkv2.rearrange("p (k s e) -> p k s e", k=HB, s=2)[:, :, 0, :]
        wv2_raw = wkv2.rearrange("p (k s e) -> p k s e", k=HB, s=2)[:, :, 1, :]
        wv2 = ctx_raw[:, 2560:2816].rearrange("p (k e) -> p k e", k=HB)
        wd2_hi, wd2_lo = parts_hi[:, 1536:2560], parts_lo[:, 1536:2560]
        c2_hi = parts_hi[:, 2560:3584].rearrange("p (b n) -> p b n", b=B)
        c2_lo = parts_lo[:, 2560:3584].rearrange("p (b n) -> p b n", b=B)
        gu_hi, gu_lo = (
            v[:].rearrange("p b i d -> p (b i d)")[:, 0:RING * HB * 2 * F].rearrange("p (s n) -> p s n", s=RING)
            for v in (ctx_hi, ctx_lo))
        dn_hi, dn_lo = (v[:].rearrange("p b i d -> p (b i d)")[:, RING * HB * 2 * F:][:, 0:RING * H]
                        .rearrange("p (s n) -> p s n", s=RING) for v in (ctx_hi, ctx_lo))
        hT_hi, hT_lo = pT_hi[:, :, 0:B * T], pT_lo[:, :, 0:B * T]
        work = probs[:].rearrange("p b j k -> p (b j k)")
        q2T = work[:, 0:1024].rearrange("p (h t) -> p h t", h=HR)
        k2T = work[:, 1024:1280]
        v2 = work[:, 1280:1536].rearrange("p (b d) -> p b d", b=B)
        p2 = work[:, 1536:2560].rearrange("p (b h k) -> p b h k", b=B, h=HR)
        p2T = work[:, 2560:3584].rearrange("p (b n) -> p b n", b=B)
        nm2 = work[:, 4608:4616].rearrange("p (b h) -> p b h", b=B)
        ds2 = work[:, 4624:4632].rearrange("p (b h) -> p b h", b=B)
        rd2 = work[:, 4640:4648].rearrange("p (b h) -> p b h", b=B)
        sg = work[:, 5120:5632].rearrange("p (s t) -> p s t", s=2)
        hT = work[:, 5632:6144].rearrange("p (s t) -> p s t", s=2)

        last_psum, last2_psum = sem("last_psum"), sem("last2_psum")
        bank = [stack.enter_context(nc.psum_tensor(f"bank{i}", [P, CH], F32)) for i in range(8)]
        S_BANK, PT_BANK, O_BANK = bank[0:2], bank[2:4], bank[4:6]
        WQK_BANK, QYO_BANK = bank[6], bank[7]
        D_LAST = (bank[7], bank[1])
        CTX_BANK = [bank[i] for i in (2, 3, 4, 5, 2, 3, 7, 2)]

        def ramp(g, n):
            return isinstance(g, int) and g == 0 and n < LAG_T

        def s_bank(g, n):
            return (bank[0], bank[1], bank[4], bank[5])[n % 4] if ramp(g, n) else S_BANK[n % 2]

        def tail(g, n):
            return isinstance(g, int) and g == G and n >= 0

        def pt_bank(g, n):
            return (bank[0], bank[2], bank[3], bank[1])[n % 4] if tail(g, n) else PT_BANK[n % 2]
        GU, DWN, LAST = bank[0:2], (bank[3], bank[4], bank[5], bank[7]), (bank[2], bank[6])

        ld_x = sem("ld_x")
        ld_ctx = [sem(f"ld_ctx{i}") for i in range(B * NCH)]
        ld_mask = [sem(f"ld_mask{b}") for b in range(B)]
        ld_wq, ld_wk, ld_wv, ld_wo = sem("ld_wq"), sem("ld_wk"), sem("ld_wv"), sem("ld_wo")
        consts = sem("consts")
        mask_ready = sem("mask_ready")
        ln_stat, ln_pow, xn_ready = sem("ln_stat"), sem("ln_pow"), sem("xn_ready")
        xnT_psum, xnT_hi_ready, xnT_ready = sem("xnT_psum"), sem("xnT_hi_ready"), sem("xnT_ready")
        xnT_whole = sem("xnT_whole")
        wq_hi_ready, wq_ready = sem("wq_hi_ready"), sem("wq_ready")
        ctxT_psum, ctxT_hi_ready, ctxT_lo_ready = sem("ctxT_psum"), sem("ctxT_hi_ready"), sem("ctxT_lo_ready")
        ctx_hi_ready, ctx_lo_ready = sem("ctx_hi_ready"), sem("ctx_lo_ready")
        wv_hi_ready, wv_ready, wo_hi_ready, wo_ready = (
            sem("wv_hi_ready"), sem("wv_ready"), sem("wo_hi_ready"), sem("wo_ready"))
        wkT_psum, wkT_hi_ready, wkT_ready = sem("wkT_psum"), sem("wkT_hi_ready"), sem("wkT_ready")
        q_psum, q_hi_ready, q_ready = sem("q_psum"), sem("q_hi_ready"), sem("q_ready")
        qk_psum, qk_hi_ready, qk_lo_ready = sem("qk_psum"), sem("qk_hi_ready"), sem("qk_lo_ready")
        scores, masked, negmax_ready, exps = sem("scores"), sem("masked"), sem("negmax_ready"), sem("exps")
        pT_psum, pT_hi_ready, pT_lo_ready = sem("pT_psum"), sem("pT_hi_ready"), sem("pT_lo_ready")
        av = sem("av")
        rden_step = sem("rden_step")
        oT_hi_ready, oT_ready, y_psum, yT_hi_ready, yT_ready, out_psum, added = (
            sem("oT_hi_ready"), sem("oT_ready"), sem("y_psum"), sem("yT_hi_ready"), sem("yT_ready"),
            sem("out_psum"), sem("added"))
        ld_wq2, ld_wkv2, ld_wd2 = sem("ld_wq2"), sem("ld_wkv2"), sem("ld_wd2")
        wq2_hi_ready, wk2_hi_ready, wd2_hi_ready = sem("wq2_hi_ready"), sem("wk2_hi_ready"), sem("wd2_hi_ready")
        wq2_ready, wk2_ready, wd2_ready = sem("wq2_ready"), sem("wk2_ready"), sem("wd2_ready")
        wv2_ready = sem("wv2_ready")
        qa_psum, qb_psum, kv2_psum = sem("qa_psum"), sem("qb_psum"), sem("kv2_psum")
        first_q, first_kv, first_qk_ready, first_qb_ready = (
            sem("first_q"), sem("first_kv"), sem("first_qk_ready"), sem("first_qb_ready"))
        qa_ready, qb_ready, k2_ready, v2_ready = sem("qa_ready"), sem("qb_ready"), sem("k2_ready"), sem("v2_ready")
        s2_psum, s2_masked, s2_negmax, s2_exps, s2_rden, s2_probs = (
            sem("s2_psum"), sem("s2_masked"), sem("s2_negmax"), sem("s2_exps"), sem("s2_rden"), sem("s2_probs"))
        p2T_psum, p2T_ready, c2_psum, c2_hi_ready, c2_ready, d2_psum, added2 = (
            sem("p2T_psum"), sem("p2T_ready"), sem("c2_psum"), sem("c2_hi_ready"), sem("c2_ready"),
            sem("d2_psum"), sem("added2"))
        ld_gate = sem("ld_gate")
        ld_gu = [sem(f"ld_gu{i}") for i in range(RING)]
        ld_dn = [sem(f"ld_dn{i}") for i in range(RING)]
        gu_hi_ready, gu_ready = sem("gu_hi_ready"), sem("gu_ready")
        dn_hi_ready, dn_ready, h_hi_ready, h_lo_ready = (
            sem("dn_hi_ready"), sem("dn_ready"), sem("h_hi_ready"), sem("h_lo_ready"))
        logits, gate_exp, route_step = sem("logits"), sem("gate_exp"), sem("route_step")
        gu_psum, silu_ready, h_ready, down_psum, added3 = (
            sem("gu_psum"), sem("silu_ready"), sem("h_ready"), sem("down_psum"), sem("added3"))
        stored = sem("stored")

        block = stack.enter_context(nc.Block())

        @block.sync
        def _(sp):
            sp.dma_start(resid[:], x_v).then_inc(ld_x, 16)

            def load_q(g):
                after(sp, wq_ready, g)
                sp.dma_start(wq[:], xq_v[g]).then_inc(ld_wq, 16)
                after(sp, wkT_psum, g)
                sp.dma_start(wk[:], xk_v[g]).then_inc(ld_wk, 16)

            def load_o(g):
                after(sp, wo_ready, g)
                sp.dma_start(wv[:], xv_v[g]).then_inc(ld_wv, 16)
                sp.dma_start(wo[:], xo_v[g]).then_inc(ld_wo, 16)

            def load_mask(b):
                sp.dma_start(mask8[:, b, :], key_mask[b:b + 1, :].broadcast_to([P, KEYS])).then_inc(ld_mask[b], 16)

            def load_ctx(c):
                b, k = divmod(c, NCH)
                sp.dma_start(ctx_raw[:, c * CH:(c + 1) * CH], ctx_v[b, :, k * CH:(k + 1) * CH]).then_inc(ld_ctx[c], 16)

            load_q(0)
            load_mask(0)
            for c in range(1, B * NCH):
                load_ctx(c)
            load_mask(1)
            load_o(0)
            sp.dma_start(gatew[:], gate_w.rearrange("(k p) e -> p k e", p=P)).then_inc(ld_gate, 16)
            sp.dma_start(bias_b[:, 0, :], expert_bias.rearrange("(a e) -> a e", a=1).broadcast_to([P, E])
                         ).then_inc(ld_gate, 16)
            load_q(1)
            with sp.Fori(1, G - 1) as g:
                load_q(g + 1)
                load_o(g)
            load_o(G - 1)

            sp.wait_ge(ctxT_psum, B * NCH)
            sp.wait_ge(ctx_hi_ready, B * NCH)
            sp.wait_ge(ctx_lo_ready, B)

            def load_qkv(r):
                after(sp, wq2_ready, r)
                sp.dma_start(wq2.rearrange("p (k e) -> p k e", k=HB), sq_v[r]).then_inc(ld_wq2, 16)
                after(sp, wv2_ready, r)
                after(sp, wk2_ready, r)
                for i in range(2):
                    sp.dma_start(wkv2.rearrange("p (k s e) -> p k s e", k=HB, s=2)[:, :, i, :],
                                 skv_v[r, i]).then_inc(ld_wkv2, 16)

            def load_d(r):
                after(sp, wd2_ready, r)
                sp.dma_start(wd2.rearrange("p (h n) -> p h n", h=HR), sd_v[r]).then_inc(ld_wd2, 16)

            load_qkv(0)
            load_d(0)
            sp.dma_start(ring_gu[:, 0, :, 0:F], sh_gate_w.rearrange("(k p) f -> p k f", p=P)).then_inc(ld_gu[0], 16)
            sp.dma_start(ring_gu[:, 0, :, F:2 * F], sh_up_w.rearrange("(k p) f -> p k f", p=P)).then_inc(ld_gu[0], 16)
            sp.dma_start(ring_dn[:, 0, :], sh_down_w).then_inc(ld_dn[0], 16)
            for m in range(1, RING):
                sp.dma_start(ring_gu[:, m], exgu_v[m - 1]).then_inc(ld_gu[m], 16)
                sp.dma_start(ring_dn[:, m, :], ex_down_w[m - 1]).then_inc(ld_dn[m], 16)
            load_qkv(1)
            with sp.Fori(1, R - 1) as r:
                load_qkv(r + 1)
                load_d(r)
            load_d(R - 1)

            def load_expert(i, s):
                m = RING * i + s
                sp.wait_ge(gu_ready, m - RING + 1)
                sp.dma_start(ring_gu[:, s], exgu_v[m - 1]).then_inc(ld_gu[s], 16)
                sp.wait_ge(dn_ready, m - RING + 1)
                sp.dma_start(ring_dn[:, s, :], ex_down_w[m - 1]).then_inc(ld_dn[s], 16)

            with sp.Fori(1, E // RING) as i:
                for s in range(RING):
                    load_expert(i, s)
            load_expert(E // RING, 0)

            for b in range(B):
                sp.wait_ge(added3, B * E + b + 1)
                sp.dma_start(out_v[:, b, :], resid[:, b, :]).then_inc(stored, 16)
            sp.wait_ge(stored, 16 * B)

        @block.gpsimd
        def _(pool):
            pool.memset(ident[:], 0.0).then_inc(consts, 1)
            pool.memset(causal[:], 0.0).then_inc(consts, 1)
            pool.memset(minus_half[:], -0.5).then_inc(consts, 1)
            pool.iota(rank[:, 0, :], [[-1, E]], base=E, channel_multiplier=0,
                      allow_small_or_imprecise_dtypes=True).then_inc(consts, 1)
            pool.wait_ge(consts, 4)
            pool.affine_select(out=ident[:], in_=ident[:], compare_op=ALU.not_equal, fill=1.0, base=0,
                               pattern=[[-1, P]], channel_multiplier=1).then_inc(consts, 1)
            pool.affine_select(out=causal[:], in_=causal[:], compare_op=ALU.is_ge, fill=NEG, base=0,
                               pattern=[[-1, P]], channel_multiplier=1).then_inc(consts, 1)
            pool.memset(ones[:], 1.0).then_inc(consts, 1)
            pool.wait_ge(consts, 7)

            def power(b, n):
                pool.wait_ge(ln_stat, 3 * (B * n + b + 1))
                pool.tensor_tensor(rstd[:, b], var_eps[:, b], minus_half[:], ALU.pow).then_inc(ln_pow, 1)

            def rest(dst, src, hi, ready):
                pool.tensor_tensor(dst, src, hi.bitcast(F32), ALU.subtract).then_inc(ready, 1)

            def split_wq(g):
                flat = "p k e -> p (k e)"
                after(pool, q_psum, g)
                pool.wait_ge(ld_wq, 16 * (g + 1))
                pool.tensor_tensor(wq_hi[:].rearrange(flat), wq[:].rearrange(flat), ones[:],
                                   ALU.mult).then_inc(wq_hi_ready, 1)
                pool.wait_ge(wq_hi_ready, g + 1)
                rest(wq_lo[:].rearrange(flat), wq[:].rearrange(flat), wq_hi[:].rearrange(flat), wq_ready)

            def split_o(g):
                after(pool, out_psum, 2 * g)
                pool.wait_ge(ld_wv, 16 * (g + 1))
                pool.tensor_tensor(wv_hi[:], wv[:], ones[:, 0:P], ALU.mult).then_inc(wv_hi_ready, 1)
                pool.wait_ge(ld_wo, 16 * (g + 1))
                pool.tensor_tensor(wo_hi[:], wo[:], ones[:].rearrange("p (j n) -> p j n", j=J),
                                   ALU.mult).then_inc(wo_hi_ready, 1)
                pool.wait_ge(wv_hi_ready, g + 1)
                rest(wv_lo[:], wv[:], wv_hi[:], wv_ready)
                pool.wait_ge(wo_hi_ready, g + 1)
                rest(wo_lo[:], wo[:], wo_hi[:], wo_ready)

            def ctx_rest(b):
                pool.wait_ge(ctx_hi_ready, NCH * (b + 1))
                rest(ctx_lo[:, b].rearrange("p i d -> p (i d)"), ctx_raw[:, b * KEYS:(b + 1) * KEYS],
                     ctx_hi[:, b].rearrange("p i d -> p (i d)"), ctx_lo_ready)

            def mask(b):
                pool.wait_ge(ld_mask[b], 16)
                for k in range(NCH):
                    pool.tensor_scalar(mask_bias[:, b, k * CH:(k + 1) * CH].rearrange("p (i q) -> p i q", q=P),
                                       mask8[:, b].rearrange("p (q i) -> p i q", i=NBLK)[:, 4 * k:4 * k + 4, :],
                                       -1.0, -NEG, ALU.add, ALU.mult).then_inc(mask_ready, 1)

            power(0, 0)
            power(1, 0)
            pool.wait_ge(wq_hi_ready, 1)
            rest(wq_lo[:], wq[:], wq_hi[:], wq_ready)
            mask(0)
            ctx_rest(0)
            split_wq(1)
            mask(1)
            ctx_rest(1)
            split_o(0)
            with pool.Fori(2, G) as g:
                split_wq(g)
                split_o(g - 1)
            split_o(G - 1)

            def split_q(r):
                pool.wait_ge(wq2_hi_ready, r + 1)
                rest(wq2_lo, wq2, wq2_hi, wq2_ready)

            def split_k(r):
                pool.wait_ge(wk2_hi_ready, r + 1)
                rest(wk2_lo, wk2, wk2_hi, wk2_ready)

            def split_d(r):
                pool.wait_ge(wd2_hi_ready, r + 1)
                rest(wd2_lo, wd2, wd2_hi, wd2_ready)

            def normalise(r):
                for b in range(B):
                    pool.wait_ge(s2_rden, 2 * r + b + 1)
                    pool.tensor_tensor(p2[:, b], p2[:, b], rd2[:, b].unsqueeze(2).broadcast_to([P, HR, P]),
                                       ALU.mult).then_inc(s2_probs, 1)

            split_q(0)
            split_k(0)
            split_d(0)
            power(0, 1)
            power(1, 1)
            split_q(1)
            split_k(1)
            normalise(0)
            split_q(2)
            split_k(2)
            with pool.Fori(1, R - 2) as r:
                normalise(r)
                split_q(r + 2)
                split_k(r + 2)
                split_d(r)
            for r in range(R - 2, R):
                normalise(r)
                split_d(r)

            def split_expert(i, s):
                pool.wait_ge(gu_hi_ready, RING * i + s + 1)
                rest(gu_lo[:, s], ring_gu[:, s].rearrange("p k f -> p (k f)"), gu_hi[:, s], gu_ready)

            split_expert(0, 0)
            split_expert(0, 1)
            for b in range(B):
                power(b, 2)
            split_expert(0, 2)
            split_expert(0, 3)

            def split_down(first):
                pool.wait_ge(dn_hi_ready, RING)
                two = slice(first, first + 2)
                pool.tensor_tensor(dn_lo[:, two], ring_dn[:, two], dn_hi[:, two].bitcast(F32),
                                   ALU.subtract).then_inc(dn_ready, 2)

            split_down(0)
            split_down(2)
            with pool.Fori(1, E // RING) as i:
                for s in range(RING):
                    split_expert(i, s)
            split_expert(E // RING, 0)

        @block.tensor
        def _(pe):
            def product(dst, w, x, start, stop):
                pe.matmul(dst, w[1], x[0], start=start, stop=False)
                pe.matmul(dst, w[0], x[1], start=False, stop=False)
                return pe.matmul(dst, w[0], x[0], start=False, stop=stop)

            def ctx_chunk(c):
                b, k = divmod(c, NCH)
                pe.wait_ge(ld_ctx[c], 16)
                if c >= 4:
                    pe.wait_ge(ctxT_lo_ready, 5 if c == 7 else 4)
                if c == 6:
                    pe.wait_ge(q_ready, 1)
                for i in range(4):
                    blk = b * NBLK + 4 * k + i
                    last = pe.transpose(CTX_BANK[c][:, i * P:(i + 1) * P], ctx_raw[:, blk * P:(blk + 1) * P], ident[:])
                last.then_inc(ctxT_psum, 1)

            def xn_transpose(b, n, dst):
                pe.wait_ge(xn_ready, B * n + b + 1)
                for k in range(HB):
                    last = pe.transpose(dst[:, k * P:(k + 1) * P], xn[:, b, k * P:(k + 1) * P], ident[:])
                last.then_inc(xnT_psum, 1)

            def wk_transpose(g):
                pe.wait_ge(ld_wk, 16 * (g + 1))
                after(pe, qk_lo_ready, 2 * g)
                pe.transpose(WQK_BANK[:, 0:P], wk[:], ident[:]).then_inc(wkT_psum, 1)

            def q_project(g, j):
                if j == 0:
                    pe.wait_ge(wq_ready, g + 1)
                for k in range(HB):
                    cols = slice(j * P, (j + 1) * P)
                    last = product(QYO_BANK[:].rearrange("p (b j t) -> p j b t", b=B, j=J)[:, j],
                                   (wq_hi[:, k, cols], wq_lo[:, k, cols]),
                                   [v[:, k, :].rearrange("p (b t) -> p b t", b=B) for v in (xnT_hi, xnT_lo)],
                                   k == 0, k == HB - 1)
                if j == J - 1:
                    last.then_inc(q_psum, 1)

            def q_fold(g):
                pe.wait_ge(wkT_ready, g + 1)
                pe.wait_ge(q_ready, g + 1)
                product(WQK_BANK[:], (wkT_hi[:], wkT_lo[:]), (qT_hi[:], qT_lo[:]), True, True).then_inc(qk_psum, 1)

            def step(g, n, scores_on, trans_on, av_on, fold_on, out_on):
                N = STEPS * g + n
                if scores_on:
                    b, j, k = n // SPU, n % SPU // NCH, n % NCH
                    if n % SPU == 0:
                        pe.wait_ge(qk_hi_ready, 2 * g + b + 1)
                        pe.wait_ge(qk_lo_ready, 2 * g + b + 1)
                    after(pe, masked, N - 3 if ramp(g, n) else N - 1)
                    keys = slice(k * CH, (k + 1) * CH)
                    pe.matmul(s_bank(g, n)[:], qk_hi[:, b, j], ctxT_lo[:, b, keys], start=True, stop=False)
                    pe.matmul(s_bank(g, n)[:], qk_lo[:, b, j], ctxT_hi[:, b, keys], start=False, stop=False)
                    pe.matmul(s_bank(g, n)[:], qk_hi[:, b, j], ctxT_hi[:, b, keys],
                              start=False, stop=True).then_inc(scores, 1)
                if trans_on:
                    t = N - LAG_T
                    p, b = (n - LAG_T) % SPU, (n - LAG_T) // SPU % 2
                    if p in (0, SPU // 2):
                        pe.wait_ge(exps, 4 * (2 * g + (n - LAG_T) // SPU) + (3 if p == 0 else 4))
                    if tail(g, n) and n in (0, 3):
                        pe.wait_ge(masked, NT - (n == 0))
                    else:
                        after(pe, pT_lo_ready, t - 1 if not tail(g, n) else t - 2 if n < 4 else t - 3)
                    for i in range(2):
                        for j in range(J):
                            at = (i * J + j) * P
                            last = pe.transpose(pt_bank(g, n)[:, at:at + P],
                                                probs[:, b, j, (2 * p + i) * P:(2 * p + i + 1) * P], ident[:])
                    last.then_inc(pT_psum, 1)
                if out_on and n in (5, 13):
                    u = 2 * (g - 1) + n // SPU
                    if n == 5:
                        pe.wait_ge(wv_ready, g)
                    pe.wait_ge(oT_ready, u + 1)
                    if not scores_on:
                        pe.wait_ge(added, 2 * u)
                    if n == 13 and fold_on:
                        pe.wait_ge(q_ready, g + 2)
                    product(QYO_BANK[:, 0:J * T], (wv_hi[:], wv_lo[:]), (oT_hi[:], oT_lo[:]),
                            True, True).then_inc(y_psum, 1)
                if out_on and n in (6, 14):
                    u = 2 * (g - 1) + n // SPU
                    if n == 6:
                        pe.wait_ge(wo_ready, g)
                    pe.wait_ge(yT_ready, u + 1)
                    for j in range(J):
                        rows = slice(j * T, (j + 1) * T)
                        last = product(QYO_BANK[:, j * H:(j + 1) * H], (yT_hi[:, rows], yT_lo[:, rows]),
                                       (wo_hi[:, j], wo_lo[:, j]), True, True)
                    last.then_inc(out_psum, 1)
                if av_on:
                    a = N - LAG_A
                    p, b = (n - LAG_A) % SPU, (n - LAG_A) // SPU % 2
                    pe.wait_ge(pT_lo_ready, a + 1)
                    s = (n - LAG_A) % PTR
                    for i in range(2):
                        blk, cols = 2 * p + i, slice(i * J * P, (i + 1) * J * P)
                        dst = O_BANK[b][:, 0:J * T]
                        pe.matmul(dst, ctx_lo[:, b, blk], pT_hi[:, s, cols], start=(blk == 0), stop=False)
                        pe.matmul(dst, ctx_hi[:, b, blk], pT_lo[:, s, cols], start=False, stop=False)
                        last = pe.matmul(dst, ctx_hi[:, b, blk], pT_hi[:, s, cols], start=False, stop=(blk == NBLK - 1))
                    last.then_inc(av, 1)
                if fold_on and n == 8:
                    wk_transpose(g + 1)
                    after(pe, added, 2 * (2 * g - 1))
                    q_project(g + 1, 0)
                if fold_on and n == 9:
                    q_project(g + 1, 1)
                if fold_on and n == 12:
                    q_fold(g + 1)

            pe.wait_ge(consts, 7)
            pe.matmul(QYO_BANK[:], ones[:, 0:P], ones[:], start=True, stop=True)
            ctx_chunk(0)
            for b in range(B):
                xn_transpose(b, 0, S_BANK[b])
            wk_transpose(0)
            ctx_chunk(1)
            pe.wait_ge(xnT_ready, B)
            q_project(0, 0)
            q_project(0, 1)
            ctx_chunk(2)
            ctx_chunk(3)
            q_fold(0)

            for n in range(STEPS):
                if n % SPU < NCH:
                    pe.wait_ge(ctxT_lo_ready, n // SPU * NCH + n % SPU + 1)
                if n == LAG_A:
                    pe.wait_ge(ctx_lo_ready, 1)
                step(0, n, True, n >= LAG_T, n >= LAG_A, True, False)
                if n < NCH:
                    ctx_chunk(NCH + n)
            pe.wait_ge(ctx_lo_ready, B)
            with pe.Fori(1, G - 1) as g:
                for n in range(STEPS):
                    step(g, n, True, True, True, True, True)
            for n in range(STEPS):
                step(G - 1, n, True, True, True, False, True)
            QA, QB, KV, D_BANK = bank[0], bank[1], bank[2], bank[7]
            SC, PC = bank[3:5], bank[5:7]
            XT = [(xnT_hi[:, k, :], xnT_lo[:, k, :]) for k in range(HB)]

            def keep_warm(where, count):
                for _ in range(count):
                    pe.matmul(where[:], pT_hi[:, 0, 0:P], pT_hi[:, 0], start=True, stop=True)

            def query(head, cols, done):
                dst, h = (QA, QB)[head // 2], head % 2
                for k in range(HB):
                    at = (k * HR + head) * P
                    last = product(dst[:, h * B * T + cols.start:h * B * T + cols.stop],
                                   (wq2_hi[:, at:at + P], wq2_lo[:, at:at + P]),
                                   [v[:, cols] for v in XT[k]], k == 0, k == HB - 1)
                if h == 1:
                    last.then_inc(done, 1)

            def queries2(r, cols):
                pe.wait_ge(wq2_ready, r + 1)
                for head in range(HR):
                    query(head, cols, (qa_psum, qb_psum)[head // 2])

            def keys_values2(r, cols, done):
                pe.wait_ge(wk2_ready, r + 1)
                pe.wait_ge(wv2_ready, r + 1)
                after(pe, v2_ready, r)
                for k in range(HB):
                    product(KV[:, cols], (wk2_hi[:, k], wk2_lo[:, k]), [v[:, cols] for v in XT[k]],
                            k == 0, k == HB - 1)
                if isinstance(r, int) and r == 0:
                    pe.wait_ge(xnT_whole, cols.stop // T)
                for b in range(cols.start // T, cols.stop // T):
                    for k in range(HB):
                        last = pe.matmul(KV[:, (B + b) * P:(B + b + 1) * P], xnT[:, k, b * T:(b + 1) * T],
                                         wv2[:, k], start=(k == 0), stop=(k == HB - 1))
                last.then_inc(done, 1)

            def scores2(r, b):
                for h in range(HR):
                    mm = pe.matmul(SC[b][:, h * P:(h + 1) * P], q2T[:, h, b * T:(b + 1) * T],
                                   k2T[:, b * T:(b + 1) * T], start=True, stop=True)
                mm.then_inc(s2_psum, 1)

            def attend2(r):
                pe.wait_ge(v2_ready, r + 1)
                for b in range(B):
                    pe.wait_ge(p2T_ready, 2 * r + b + 1)
                    pe.matmul(PC[b][:], v2[:, b], p2T[:, b], start=True, stop=True).then_inc(c2_psum, 1)

            def dense2(r, last=False):
                pe.wait_ge(wd2_ready, r + 1)
                for b in range(B):
                    pe.wait_ge(c2_ready, 2 * r + b + 1)
                    for h in range(HR):
                        cols = slice(h * P, (h + 1) * P)
                        dst = D_LAST[b] if last else D_BANK
                        mm = product(dst[:, b * H:(b + 1) * H], (c2_hi[:, b, cols], c2_lo[:, b, cols]),
                                     (wd2_hi[:, h * H:(h + 1) * H], wd2_lo[:, h * H:(h + 1) * H]),
                                     h == 0, h == HR - 1)
                    if last:
                        mm.then_inc(last2_psum, 1)
                if not last:
                    mm.then_inc(d2_psum, 1)

            def group2(r, before, behind):
                pe.wait_ge(qa_ready, r + 1)
                pe.wait_ge(qb_ready, r + 1)
                pe.wait_ge(k2_ready, r + 1)
                for b in range(0 if before else 1, B):
                    scores2(r, b)
                if before:
                    attend2(r - 1)
                if not behind:
                    keep_warm(QA, 8)
                if behind:
                    queries2(r + 1, both)
                if before:
                    dense2(r - 1)
                if behind:
                    keys_values2(r + 1, both, kv2_psum)
                for b in range(B):
                    pe.wait_ge(s2_probs, 2 * r + b + 1)
                    for h in range(HR):
                        mm = pe.transpose(PC[b][:, h * P:(h + 1) * P], p2[:, b, h], ident[:])
                    mm.then_inc(p2T_psum, 1)

            both, of = slice(0, B * T), [slice(b * T, (b + 1) * T) for b in range(B)]
            for n in range(STEPS):
                step(G, n, False, n < LAG_T, n < LAG_A, False, True)
                if n == LAG_T:
                    xn_transpose(0, 1, WQK_BANK)
                if n == LAG_A - 1:
                    pe.wait_ge(masked, NT)
                    pe.wait_ge(xnT_ready, B + 1)
                    pe.wait_ge(wq2_ready, 1)
                    query(0, of[0], first_q)
                if n == 13:
                    query(1, of[0], first_q)
                    query(2, of[0], first_q)
                if n == 14:
                    query(3, of[0], first_q)
                    keys_values2(0, of[0], first_kv)
                    keep_warm(bank[4], 2)
            pe.wait_ge(first_qk_ready, 2)
            pe.wait_ge(first_qb_ready, 1)
            scores2(0, 0)
            keep_warm(bank[4], 1)
            xn_transpose(1, 1, WQK_BANK)
            keep_warm(bank[4], 5)
            pe.wait_ge(xnT_ready, 2 * B)
            queries2(0, of[1])
            keys_values2(0, of[1], kv2_psum)
            group2(0, False, True)
            with pe.Fori(1, R - 1) as r:
                group2(r, True, True)
            group2(R - 1, True, False)
            keep_warm(QA, 2)
            attend2(R - 1)
            keep_warm(QA, 4)
            dense2(R - 1, last=True)
            keep_warm(QA, 9)

            for b in range(B):
                xn_transpose(b, 2, (bank[2], bank[5])[b])
            keep_warm(QA, 5)
            pe.wait_ge(xnT_ready, 3 * B)

            def gate_up(i, s):
                m = RING * i + s
                pe.wait_ge(gu_ready, m + 1)
                after(pe, h_ready, m - 1)
                for half in range(2):
                    for k in range(HB):
                        at = (2 * k + half) * F
                        mm = product(GU[s % 2][:, half * B * T:(half + 1) * B * T],
                                     (gu_hi[:, s, at:at + F], gu_lo[:, s, at:at + F]), XT[k], k == 0, k == HB - 1)
                mm.then_inc(gu_psum, 1)

            def down(i, s):
                m = RING * i + s
                pe.wait_ge(dn_ready, m + 1)
                pe.wait_ge(h_lo_ready, m + 1)
                after(pe, added3, B * (m - (RING if isinstance(m, int) else 2) + 1))
                for b in range(B):
                    rows = slice(b * T, (b + 1) * T)
                    mm = product(DWN[s][:, b * H:(b + 1) * H], (hT_hi[:, s, rows], hT_lo[:, s, rows]),
                                 (dn_hi[:, s], dn_lo[:, s]), True, True)
                mm.then_inc(down_psum, 1)

            pe.wait_ge(ld_gate, 32)
            for b in range(B):
                pe.wait_ge(xnT_whole, B + b + 1)
                for k in range(HB):
                    mm = pe.matmul(bank[6][:, b * E:(b + 1) * E], xnT[:, k, b * T:(b + 1) * T], gatew[:, k, :],
                                   start=(k == 0), stop=(k == HB - 1))
            mm.then_inc(logits, 1)
            gate_up(0, 0)
            for s in range(1, RING):
                gate_up(0, s)
                if s >= 2:
                    down(0, s - 2)
            with pe.Fori(1, E // RING) as i:
                for s in range(RING):
                    gate_up(i, s)
                    if s < 2:
                        down(i - 1, s + 2)
                    else:
                        down(i, s - 2)
            gate_up(E // RING, 0)
            down(E // RING - 1, 2)
            down(E // RING - 1, 3)
            pe.wait_ge(ld_dn[0], 16 * (E // RING + 1))
            pe.wait_ge(h_ready, E + 1)
            for b in range(B):
                pe.matmul(LAST[b][:, 0:H], hT[:, 0, b * T:(b + 1) * T], ring_dn[:, 0, :],
                          start=True, stop=True).then_inc(last_psum, 1)

        @block.scalar
        def _(act):
            act.preload_act_table(ACT.Exp)
            act.dma_start(ctx_raw[:, 0:CH], ctx_v[0, :, 0:CH]).then_inc(ld_ctx[0], 16)

            def ctx_chunk(c):
                b, k = divmod(c, NCH)
                act.wait_ge(ctxT_psum, c + 1)
                act.activation(ctxT_hi[:, b, k * CH:(k + 1) * CH], CTX_BANK[c][:], ACT.Copy).then_inc(ctxT_hi_ready, 1)

            def ctx_round(c):
                b, k = divmod(c, NCH)
                act.wait_ge(ld_ctx[c], 16)
                act.activation(ctx_hi[:, b, 4 * k:4 * k + 4].rearrange("p i d -> p (i d)"),
                               ctx_raw[:, c * CH:(c + 1) * CH], ACT.Copy).then_inc(ctx_hi_ready, 1)

            def xnT_copy(b, n, src):
                act.wait_ge(xnT_psum, B * n + b + 1)
                rows = src[:, 0:HB * P].rearrange("p (k t) -> p k t", k=HB)
                act.activation(xnT_hi[:, :, b * T:(b + 1) * T], rows, ACT.Copy).then_inc(xnT_hi_ready, 1)
                return rows

            def xnT_copy_whole(b, n, rows):
                act.wait_ge(xnT_ready, B * n + b + 1)
                act.activation(xnT[:, :, b * T:(b + 1) * T], rows, ACT.Copy).then_inc(xnT_whole, 1)

            def wkT_copy(g):
                act.wait_ge(wkT_psum, g + 1)
                act.activation(wkT_hi[:], WQK_BANK[:, 0:P], ACT.Copy).then_inc(wkT_hi_ready, 1)

            def q_copy(g):
                act.wait_ge(q_psum, g + 1)
                act.activation(qT_hi[:], QYO_BANK[:], ACT.Copy).then_inc(q_hi_ready, 1)

            def fold_copy(g, b):
                if b == 0:
                    act.wait_ge(qk_psum, g + 1)
                else:
                    act.wait_ge(qk_lo_ready, 2 * g + 1)
                after(act, scores, STEPS * (g - 1) + SPU * (b + 1))
                act.activation(qk_hi[:, b].rearrange("p j t -> p (j t)"), WQK_BANK[:, b * J * T:(b + 1) * J * T],
                               ACT.Copy).then_inc(qk_hi_ready, 1)

            def exp_half(g, du, j, half):
                u = 2 * g + du
                b = du % 2
                if half == 0:
                    act.wait_ge(negmax_ready, 2 * u + j + 1)
                part = probs[:, b, j, half * (KEYS // 2):(half + 1) * (KEYS // 2)]
                act.activation(part, part, ACT.Exp, bias=negmax[:, b, j:j + 1], scale=SCALE,
                               accum_out=den[:, b, j, half:half + 1]).then_inc(exps, 1)

            EXPS = {1: (-1, 1, 0), 3: (-1, 1, 1), 5: (0, 0, 0), 7: (0, 0, 1),
                    9: (0, 1, 0), 11: (0, 1, 1), 13: (1, 0, 0), 15: (1, 0, 1)}

            def step(g, n, exp_on, trans_on, fold_on, fold2_on, out_on):
                t = STEPS * g + n - LAG_T
                if out_on and n in (4, 12):
                    u = 2 * (g - 1) + n // SPU
                    act.wait_ge(av, SPU * (u + 1))
                    act.activation(oT_hi[:], O_BANK[n // SPU][:, 0:J * T], ACT.Copy).then_inc(oT_hi_ready, 1)
                if out_on and n in (5, 13):
                    u = 2 * (g - 1) + n // SPU
                    act.wait_ge(y_psum, u + 1)
                    act.activation(yT_hi[:], QYO_BANK[:, 0:J * T], ACT.Copy).then_inc(yT_hi_ready, 1)
                if exp_on and n in EXPS:
                    exp_half(g, *EXPS[n])
                if trans_on:
                    after(act, av, t - PTR + 1)
                    act.wait_ge(pT_psum, t + 1)
                    act.activation(pT_hi[:, (n - LAG_T) % PTR], pt_bank(g, n)[:], ACT.Copy).then_inc(pT_hi_ready, 1)
                if fold2_on and n == 0:
                    fold_copy(g, 1)
                if fold_on and n == 9:
                    wkT_copy(g + 1)
                if fold_on and n == 10:
                    q_copy(g + 1)
                if fold_on and n == 13:
                    fold_copy(g + 1, 0)

            act.wait_ge(ld_wq, 16)
            act.activation(wq_hi[:], wq[:], ACT.Copy).then_inc(wq_hi_ready, 1)
            ctx_chunk(0)
            for b in range(B):
                xnT_copy(b, 0, S_BANK[b])
            wkT_copy(0)
            ctx_chunk(1)
            ctx_round(0)
            q_copy(0)
            ctx_chunk(2)
            ctx_chunk(3)
            fold_copy(0, 0)
            for c in range(1, NCH):
                ctx_round(c)

            for n in range(STEPS):
                if n < NCH:
                    step(0, n, False, False, True, True, False)
                    ctx_chunk(NCH + n)
                    ctx_round(NCH + n)
                else:
                    step(0, n, n >= 5, n >= LAG_T, True, True, False)
            with act.Fori(1, G - 1) as g:
                for n in range(STEPS):
                    step(g, n, True, True, True, True, True)
            for n in range(STEPS):
                step(G - 1, n, True, True, False, True, True)
            QA, KV, PC = bank[0], bank[2], bank[5:7]

            def q_half(cols):
                return QA[:].rearrange("p (h t) -> p h t", h=2)[:, :, cols]

            def copy_qk(r):
                after(act, s2_psum, 2 * r)
                act.wait_ge(qa_psum, r + 1)
                act.activation(q2T[:, 0:2].rearrange("p h t -> p (h t)"), QA[:], ACT.Copy).then_inc(qa_ready, 1)
                act.wait_ge(kv2_psum, r + 1)
                act.activation(k2T, KV[:, 0:B * T], ACT.Copy).then_inc(k2_ready, 1)

            def exps2(r, b):
                act.wait_ge(s2_negmax, 2 * r + b + 1)
                for h in range(HR):
                    act.activation(p2[:, b, h], p2[:, b, h], ACT.Exp, bias=nm2[:, b, h:h + 1],
                                   accum_out=ds2[:, b, h:h + 1]).then_inc(s2_exps, 1)

            def copy_c(r):
                for b in range(B):
                    act.wait_ge(c2_psum, 2 * r + b + 1)
                    act.activation(c2_hi[:, b], PC[b][:], ACT.Copy).then_inc(c2_hi_ready, 1)

            def group2(r, before, behind):
                if before:
                    exps2(r, 0)
                if before:
                    copy_c(r - 1)
                exps2(r, 1)
                if behind:
                    copy_qk(r + 1)
                for b in range(B):
                    act.wait_ge(p2T_psum, 2 * r + b + 1)
                    act.activation(p2T[:, b], PC[b][:], ACT.Copy).then_inc(p2T_ready, 1)

            for n in range(STEPS):
                step(G, n, n < 5, n < LAG_T, False, False, True)
                if n == LAG_T:
                    xnT_rows = xnT_copy(0, 1, WQK_BANK)
                if n == LAG_A:
                    xnT_copy_whole(0, 1, xnT_rows)
                if n == 14:
                    act.wait_ge(first_q, 1)
                    act.activation(q2T[:, 0:2, 0:T], q_half(slice(0, T)), ACT.Copy).then_inc(first_qk_ready, 1)
            act.wait_ge(first_kv, 1)
            act.activation(k2T[:, 0:T], KV[:, 0:T], ACT.Copy).then_inc(first_qk_ready, 1)
            xnT_rows = xnT_copy(1, 1, WQK_BANK)
            exps2(0, 0)
            xnT_copy_whole(1, 1, xnT_rows)
            act.wait_ge(qa_psum, 1)
            act.activation(q2T[:, 0:2, T:2 * T], q_half(slice(T, 2 * T)), ACT.Copy).then_inc(qa_ready, 1)
            act.wait_ge(kv2_psum, 1)
            act.activation(k2T[:, T:2 * T], KV[:, T:2 * T], ACT.Copy).then_inc(k2_ready, 1)
            group2(0, False, True)
            with act.Fori(1, R - 1) as r:
                group2(r, True, True)
            group2(R - 1, True, False)
            copy_c(R - 1)
            for s in range(RING):
                act.wait_ge(ld_dn[s], 16)
                act.activation(dn_hi[:, s], ring_dn[:, s], ACT.Copy).then_inc(dn_hi_ready, 1)

            def silu(m, s):
                after(act, h_ready, m - 1)
                act.wait_ge(gu_psum, m + 1)
                act.activation(sg[:, s % 2], GU[s % 2][:, 0:B * T], ACT.Silu).then_inc(silu_ready, 1)

            rows = [xnT_copy(b, 2, (bank[2], bank[5])[b]) for b in range(B)]
            for b in range(B):
                xnT_copy_whole(b, 2, rows[b])
            act.wait_ge(logits, 1)
            act.activation(sc.rearrange("p b e -> p (b e)"), bank[6][:, 0:B * E], ACT.Exp,
                           scale=-1.0).then_inc(gate_exp, 1)
            def round_gu(m, s, fill):
                act.wait_ge(gu_psum, m - RING + 1)
                act.wait_ge(ld_gu[s], fill)
                act.activation(gu_hi[:, s], ring_gu[:, s].rearrange("p k f -> p (k f)"),
                               ACT.Copy).then_inc(gu_hi_ready, 1)

            def round_dn(m, s, fill):
                act.wait_ge(down_psum, m - RING + 1)
                act.wait_ge(ld_dn[s], fill)
                act.activation(dn_hi[:, s], ring_dn[:, s], ACT.Copy).then_inc(dn_hi_ready, 1)

            def unit(i, s, gu_on, dn_on):
                m = RING * i + s
                silu(m, s)
                if gu_on:
                    t, turn = (s + 3) % RING, i + (s + 3) // RING
                    round_gu(m + 3, t, 16 * turn + (32 if t == 0 else 16))
                act.wait_ge(h_ready, m + 1)
                act.activation(hT_hi[:, s], hT[:, s % 2], ACT.Copy).then_inc(h_hi_ready, 1)
                if dn_on:
                    t, turn = (s + 1) % RING, i + (s + 1) // RING
                    round_dn(m + 1, t, 16 * (turn + 1))

            for s in range(RING):
                unit(0, s, s >= 1, s == RING - 1)
            with act.Fori(1, E // RING - 1) as i:
                for s in range(RING):
                    unit(i, s, True, True)
            for s in range(RING):
                unit(E // RING - 1, s, s < 2, s < RING - 1)
            silu(E, 0)

        @block.vector
        def _(dve):
            def norm_stats(b, n):
                o = 3 * (B * n + b)
                dve.bn_stats(stats[:, b, :], resid[:, b, :]).then_inc(ln_stat, 1)
                dve.wait_ge(ln_stat, o + 1)
                dve.bn_aggr(meanvar[:, b, :], stats[:, b, :]).then_inc(ln_stat, 1)
                dve.wait_ge(ln_stat, o + 2)
                dve.tensor_scalar(var_eps[:, b], meanvar[:, b, 1:2], EPS, None, ALU.add).then_inc(ln_stat, 1)

            def norm_apply(b, n):
                dve.wait_ge(ln_pow, B * n + b + 1)
                after(dve, xnT_psum, B * (n - 1) + b + 1)
                dve.tensor_scalar(xn[:, b, :], resid[:, b, :], meanvar[:, b, 0:1], rstd[:, b],
                                  ALU.subtract, ALU.mult).then_inc(xn_ready, 1)

            def xnT_rest(b, n, src):
                dve.wait_ge(xnT_hi_ready, B * n + b + 1)
                dve.tensor_tensor(xnT_lo[:, :, b * T:(b + 1) * T], src[:, 0:HB * P].rearrange("p (k t) -> p k t", k=HB),
                                  xnT_hi[:, :, b * T:(b + 1) * T].bitcast(F32), ALU.subtract).then_inc(xnT_ready, 1)

            def ctx_chunk(c):
                b, k = divmod(c, NCH)
                dve.wait_ge(ctxT_hi_ready, c + 1)
                cols = slice(k * CH, (k + 1) * CH)
                dve.tensor_tensor(ctxT_lo[:, b, cols], CTX_BANK[c][:], ctxT_hi[:, b, cols].bitcast(F32),
                                  ALU.subtract).then_inc(ctxT_lo_ready, 1)

            def fold_rest(g, b):
                dve.wait_ge(qk_hi_ready, 2 * g + b + 1)
                dve.tensor_tensor(qk_lo[:, b].rearrange("p j t -> p (j t)"), WQK_BANK[:, b * J * T:(b + 1) * J * T],
                                  qk_hi[:, b].bitcast(F32).rearrange("p j t -> p (j t)"),
                                  ALU.subtract).then_inc(qk_lo_ready, 1)

            def rest_of(lo, src, hi, hi_ready, count, ready):
                dve.wait_ge(hi_ready, count + 1)
                dve.tensor_tensor(lo[:], src[:, 0:lo.shape[1]], hi[:].bitcast(F32), ALU.subtract).then_inc(ready, 1)

            def wkT_rest(g):
                rest_of(wkT_lo, WQK_BANK, wkT_hi, wkT_hi_ready, g, wkT_ready)

            def q_rest(g):
                rest_of(qT_lo, QYO_BANK, qT_hi, q_hi_ready, g, q_ready)

            def denominators(g, du):
                u, b = 2 * g + du, du % 2
                dve.wait_ge(exps, 4 * u + 4)
                dve.tensor_tensor(dsum[:, b], den[:, b, :, 0], den[:, b, :, 1], ALU.add).then_inc(rden_step, 1)
                dve.wait_ge(rden_step, 3 * u + 1)
                dve.reciprocal(dsum[:, b], dsum[:, b]).then_inc(rden_step, 1)
                dve.wait_ge(rden_step, 3 * u + 2)
                dve.scalar_tensor_tensor(rden[:, b], rmax[:, b, :, NCH - 1], NEG / 2, dsum[:, b],
                                         ALU.is_gt, ALU.mult).then_inc(rden_step, 1)

            EDGE = 9

            def step(g, n, scores_on, trans_on, fold_on, fold2_on, rden_on, out_on):
                N = STEPS * g + n
                t = N - 1 - LAG_T
                if scores_on:
                    b, j, k = n // SPU, n % SPU // NCH, n % NCH
                    dve.wait_ge(scores, N + 1)
                    after(dve, masked, N)
                if trans_on:
                    dve.wait_ge(pT_hi_ready, t + 1)
                    dve.tensor_tensor(pT_lo[:, (n - 1 - LAG_T) % PTR], pt_bank(g, n - 1)[:],
                                      pT_hi[:, (n - 1 - LAG_T) % PTR].bitcast(F32),
                                      ALU.subtract).then_inc(pT_lo_ready, 1)
                if scores_on:
                    keys = slice(k * CH, (k + 1) * CH)
                    dve.tensor_tensor_reduce(out=probs[:, b, j, keys], in0=s_bank(g, n)[:], in1=mask_bias[:, b, keys],
                                             scale=1.0, scalar=(NEG if k == 0 else rmax[:, b, j, k - 1:k]),
                                             op0=ALU.add, op1=ALU.max,
                                             accum_out=rmax[:, b, j, k:k + 1]).then_inc(masked, 1)
                    if k == NCH - 1:
                        dve.wait_ge(masked, N + 1)
                        dve.tensor_scalar(negmax[:, b, j:j + 1], rmax[:, b, j, k:k + 1], -SCALE, None,
                                          ALU.mult).then_inc(negmax_ready, 1)
                if fold2_on and n == 1:
                    fold_rest(g, 1)
                if fold_on and n == 14:
                    fold_rest(g + 1, 0)
                if fold_on and n == 9:
                    wkT_rest(g + 1)
                if fold_on and n == 11:
                    q_rest(g + 1)
                if out_on and n in (4, 12):
                    u = 2 * (g - 1) + n // SPU
                    rest_of(oT_lo, O_BANK[n // SPU], oT_hi, oT_hi_ready, u, oT_ready)
                if out_on and n in (5, 13):
                    u = 2 * (g - 1) + n // SPU
                    rest_of(yT_lo, QYO_BANK, yT_hi, yT_hi_ready, u, yT_ready)
                if rden_on and n == 5:
                    denominators(g, -1)
                if rden_on and n == 13:
                    denominators(g, 0)
                if out_on and n in (6, 14):
                    b = n // SPU
                    u = 2 * (g - 1) + b
                    dve.wait_ge(out_psum, u + 1)
                    for j in range(J):
                        if j:
                            dve.wait_ge(added, 2 * u + 1)
                        dve.scalar_tensor_tensor(resid[:, b, :], QYO_BANK[:, j * H:(j + 1) * H], rden[:, b, j:j + 1],
                                                 resid[:, b, :], ALU.mult, ALU.add).then_inc(added, 1)

            QB, KV, D_BANK = bank[1], bank[2], bank[7]
            SC, PC = bank[3:5], bank[5:7]

            def first_qb(b, done, count, ready):
                cols = slice(b * T, (b + 1) * T)
                dve.wait_ge(done, count)
                dve.tensor_copy(q2T[:, 2:4, cols],
                                QB[:].rearrange("p (h t) -> p h t", h=2)[:, :, cols]).then_inc(ready, 1)

            def scale2(r, b):
                dve.wait_ge(s2_psum, 2 * r + b + 1)
                dve.scalar_tensor_tensor(p2[:, b], SC[b][:].rearrange("p (h k) -> p h k", h=HR), SCALE,
                                         causal[:].unsqueeze(1).broadcast_to([P, HR, P]),
                                         ALU.mult, ALU.add).then_inc(s2_masked, 1)

            def max2(r, b):
                dve.wait_ge(s2_masked, 2 * r + b + 1)
                dve.tensor_reduce(nm2[:, b], p2[:, b], AX.X, ALU.max, negate=True).then_inc(s2_negmax, 1)

            def round_to(hi, raw, ready):
                dve.tensor_copy(hi, raw).then_inc(ready, 1)

            def round_q(r):
                after(dve, qb_psum, r)
                dve.wait_ge(ld_wq2, 16 * (r + 1))
                round_to(wq2_hi, wq2, wq2_hi_ready)

            def round_kv(r):
                after(dve, kv2_psum, r)
                dve.wait_ge(ld_wkv2, 32 * (r + 1))
                round_to(wk2_hi, wk2, wk2_hi_ready)
                dve.tensor_copy(wv2, wv2_raw).then_inc(wv2_ready, 1)

            def round_d(r):
                after(dve, d2_psum, r)
                dve.wait_ge(ld_wd2, 16 * (r + 1))
                round_to(wd2_hi, wd2, wd2_hi_ready)

            dve.wait_ge(ld_x, 16)
            norm_stats(0, 0)
            norm_stats(1, 0)
            norm_apply(0, 0)
            norm_apply(1, 0)
            for b in range(B):
                xnT_rest(b, 0, S_BANK[b])
            ctx_chunk(0)
            wkT_rest(0)
            ctx_chunk(1)
            q_rest(0)
            ctx_chunk(2)
            ctx_chunk(3)
            fold_rest(0, 0)

            for n in range(STEPS):
                if n % SPU < NCH:
                    dve.wait_ge(mask_ready, n // SPU * NCH + n % SPU + 1)
                step(0, n, True, n > LAG_T, True, True, n == 13, False)
                if n < NCH:
                    ctx_chunk(NCH + n)
            for n in range(EDGE):
                step(1, n, True, True, True, True, True, True)
            with dve.Fori(1, G - 1) as g:
                for n in range(EDGE, STEPS):
                    step(g, n, True, True, True, True, True, True)
                for n in range(EDGE):
                    step(g + 1, n, True, True, True, True, True, True)
            for n in range(EDGE, STEPS):
                step(G - 1, n, True, True, False, True, True, True)
            for n in range(STEPS):
                step(G, n, False, n <= LAG_T, False, False, n == 5, True)
                if n == 3:
                    dve.wait_ge(scores, NT)
                    round_q(0)
                if n == 4:
                    round_kv(0)
                if n == 5:
                    round_d(0)
                if n in (7, 15):
                    b = n // SPU
                    dve.wait_ge(added, 2 * (2 * (G - 1) + b + 1))
                    norm_stats(b, 1)
                if n == 8:
                    norm_apply(0, 1)
                if n == LAG_T:
                    xnT_rest(0, 1, WQK_BANK)
            first_qb(0, first_q, 2, first_qb_ready)
            norm_apply(1, 1)
            scale2(0, 0)
            max2(0, 0)
            xnT_rest(1, 1, WQK_BANK)
            first_qb(1, qb_psum, 1, qb_ready)

            def copy_qb(r):
                after(dve, s2_psum, 2 * r)
                dve.wait_ge(qb_psum, r + 1)
                dve.tensor_copy(q2T[:, 2:4].rearrange("p h t -> p (h t)"), QB[:]).then_inc(qb_ready, 1)

            def copy_v(r):
                after(dve, c2_psum, 2 * r)
                dve.wait_ge(k2_ready, r + 1)
                dve.tensor_copy(v2.rearrange("p b d -> p (b d)"), KV[:, B * P:2 * B * P]).then_inc(v2_ready, 1)

            def rest_c(r):
                for b in range(B):
                    dve.wait_ge(c2_hi_ready, 2 * r + b + 1)
                    dve.tensor_tensor(c2_lo[:, b], PC[b][:], c2_hi[:, b].bitcast(F32),
                                      ALU.subtract).then_inc(c2_ready, 1)

            def add2(r):
                dve.wait_ge(d2_psum, r + 1)
                rows = resid[:].rearrange("p b n -> p (b n)")
                dve.tensor_tensor(rows, D_BANK[:], rows, ALU.add).then_inc(added2, 1)

            def group2(r, before, behind, split):
                for b in range(0 if before else 1, B):
                    scale2(r, b)
                    max2(r, b)
                copy_v(r)
                if before:
                    rest_c(r - 1)
                for b in range(B):
                    dve.wait_ge(s2_exps, HR * (2 * r + b + 1))
                    dve.reciprocal(rd2[:, b], ds2[:, b]).then_inc(s2_rden, 1)
                if split:
                    round_q(r + 2)
                if before:
                    add2(r - 1)
                if behind:
                    copy_qb(r + 1)
                if split:
                    round_kv(r + 2)
                if before:
                    round_d(r)

            round_q(1)
            round_kv(1)
            group2(0, False, True, True)
            with dve.Fori(1, R - 2) as r:
                group2(r, True, True, True)
            group2(R - 2, True, True, False)
            group2(R - 1, True, False, False)


            for s in range(RING):
                dve.wait_ge(ld_gu[s], 32 if s == 0 else 16)
                dve.tensor_copy(gu_hi[:, s], ring_gu[:, s].rearrange("p k f -> p (k f)")).then_inc(gu_hi_ready, 1)
            rest_c(R - 1)
            for b in range(B):
                dve.wait_ge(last2_psum, b + 1)
                dve.wait_ge(added2, R - 1)
                dve.tensor_tensor(resid[:, b, :], D_LAST[b][:, b * H:(b + 1) * H], resid[:, b, :],
                                  ALU.add).then_inc(added2, 1)
                dve.wait_ge(added2, R + b)
                norm_stats(b, 2)
            for b in range(B):
                norm_apply(b, 2)
            for b in range(B):
                xnT_rest(b, 2, (bank[2], bank[5])[b])

            biased, eq, cand, hot1, hot2, comb = (route[:, i] for i in range(1, 7))
            top1, at1, top2, at2, total, rtotal = (r1[:, i] for i in range(6))

            def wide(v):
                return v.broadcast_to([P, B, E])

            flow = [0]

            def chained(ins):
                flow[0] += 1
                ins.then_inc(route_step, 1)
                dve.wait_ge(route_step, flow[0])

            def gated(m, s):
                dve.wait_ge(silu_ready, m + 1)
                dve.tensor_tensor(hT[:, s % 2], GU[s % 2][:, B * T:2 * B * T], sg[:, s % 2],
                                  ALU.mult).then_inc(h_ready, 1)

            def rest_h(m, s):
                dve.wait_ge(h_hi_ready, m + 1)
                dve.tensor_tensor(hT_lo[:, s], hT[:, s % 2], hT_hi[:, s].bitcast(F32),
                                  ALU.subtract).then_inc(h_lo_ready, 1)

            def router():
                dve.wait_ge(gate_exp, 1)
                chained(dve.tensor_scalar(sc, sc, 1.0, None, ALU.add))
                chained(dve.reciprocal(sc, sc))
                chained(dve.tensor_tensor(biased, sc, bias_b[:].broadcast_to([P, B, E]), ALU.add))
                for top, at, hot in ((top1, at1, hot1), (top2, at2, hot2)):
                    chained(dve.tensor_reduce(top, biased, AX.X, ALU.max))
                    chained(dve.tensor_tensor(eq, biased, wide(top), ALU.is_equal))
                    chained(dve.tensor_tensor(cand, eq, rank[:].broadcast_to([P, B, E]), ALU.mult))
                    chained(dve.tensor_reduce(at, cand, AX.X, ALU.max))
                    chained(dve.tensor_tensor(hot, cand, wide(at), ALU.is_equal))
                    if hot is hot2:
                        rest_h(0, 0)
                    gated(*((0, 0) if hot is hot1 else (1, 1)))
                    if hot is hot1:
                        chained(dve.scalar_tensor_tensor(biased, hot1, NEG, biased, ALU.mult, ALU.add))
                chained(dve.tensor_tensor(hot1, hot1, hot2, ALU.add))
                chained(dve.tensor_tensor(comb, hot1, sc, ALU.mult))
                chained(dve.tensor_reduce(total, comb, AX.X, ALU.add))
                chained(dve.tensor_scalar(total, total, 1e-20, None, ALU.add))
                chained(dve.reciprocal(rtotal, total))
                chained(dve.tensor_tensor(comb, comb, wide(rtotal), ALU.mult))

            def add_expert(m, s):
                dve.wait_ge(down_psum, m + 1)
                for b in range(B):
                    dve.wait_ge(added3, B * (m - 1) + b + 1)
                    dve.scalar_tensor_tensor(resid[:, b, :], DWN[s][:, b * H:(b + 1) * H],
                                             comb[:, b, bass.ds(m - 1, 1)], resid[:, b, :],
                                             ALU.mult, ALU.add).then_inc(added3, 1)

            def unit(i, s, dn_on):
                m = RING * i + s
                gated(m, s)
                if isinstance(m, int) and m == RING - 1:
                    dve.wait_ge(down_psum, 1)
                    rows = resid[:].rearrange("p b n -> p (b n)")
                    dve.tensor_tensor(rows, DWN[0][:], rows, ALU.add).then_inc(added3, B)
                elif not isinstance(m, int) or m >= RING:
                    add_expert(m - 3, (s - 3) % RING)
                rest_h(m, s)
                if dn_on:
                    dve.wait_ge(dn_hi_ready, m + 2)
                    t = (s + 1) % RING
                    dve.tensor_tensor(dn_lo[:, t], ring_dn[:, t], dn_hi[:, t].bitcast(F32),
                                      ALU.subtract).then_inc(dn_ready, 1)

            router()
            rest_h(1, 1)
            dve.wait_ge(dn_ready, RING)
            for s in range(2, RING):
                unit(0, s, s == RING - 1)
            with dve.Fori(1, E // RING - 1) as i:
                for s in range(RING):
                    unit(i, s, True)
            for s in range(RING):
                unit(E // RING - 1, s, s < RING - 1)
            add_expert(E - 3, 1)
            gated(E, 0)
            add_expert(E - 2, 2)
            add_expert(E - 1, 3)
            for b in range(B):
                dve.wait_ge(last_psum, b + 1)
                dve.wait_ge(added3, B * (E - 1) + b + 1)
                dve.scalar_tensor_tensor(resid[:, b, :], LAST[b][:, 0:H], comb[:, b, E - 1:E], resid[:, b, :],
                                         ALU.mult, ALU.add).then_inc(added3, 1)


_INS = ['x', 'ctx_1024', 'mask_BxS2_bf1', 'L0_xattn_Wq', 'L0_xattn_Wk', 'L0_xattn_Wv', 'L0_xattn_Wo',
        'L0_attn_w_q', 'L0_attn_w_kv', 'L0_attn_w_dense', 'L0_ffn_gate_w', 'L0_ffn_expert_bias',
        'L0_ffn_shared_gate_w', 'L0_ffn_shared_up_w', 'L0_ffn_shared_down_w', 'L0_ffn_experts_gate_up',
        'L0_ffn_experts_down']
_OUTS = [((2, 128, 256), 'float32')]


def kernel(**inputs):
    import numpy as _np
    import concourse.bacc as _bacc
    from concourse import mybir as _mybir
    from concourse.bass_utils import run_bass_kernel_spmd as _run

    nc = _bacc.Bacc("TRN2", target_bir_lowering=False, num_devices=1)
    arrays, args = {}, []
    for name in _INS:
        a = _np.ascontiguousarray(inputs[name])
        arrays[f"in_{name}_dram"] = a
        args.append(nc.dram_tensor(f"in_{name}_dram", a.shape, _mybir.dt.from_np(a.dtype), kind="ExternalInput").ap())
    for i, (shape, dtype) in enumerate(_OUTS):
        dt = _mybir.dt.from_np(_np.dtype(dtype))
        args.append(nc.dram_tensor(f"out_{i}_dram", shape, dt, kind="ExternalOutput").ap())
    perceiver_layer(nc, *args)
    r = _run(nc, [arrays], core_ids=[0])
    got = tuple(r.results[0][f"out_{i}_dram"] for i in range(len(_OUTS)))
    return got[0]
```
